# Optimizing a Trainium2 kernel written in Bass

```python
import numpy as np
import jax
import jax.numpy as jnp

def _softmax(x, axis=-1):
    return jax.nn.softmax(x, axis=axis)

def _gelu(x):
    return jax.nn.gelu(x, approximate=True)

def _silu(x):
    return jax.nn.silu(x)

def _sigmoid(x):
    return jax.nn.sigmoid(x)

def _layernorm(x, axis=-1, eps=1e-05):
    m = jnp.mean(x, axis=axis, keepdims=True)
    v = jnp.var(x, axis=axis, keepdims=True)
    return (x - m) / jnp.sqrt(v + eps)

def _scatter_add(tgt, idx, src, axis=0):
    return tgt.at[idx].add(src)

def _segment_sum(src, seg, n):
    return jax.ops.segment_sum(src, seg, n)
kernel_name = 'mk_macaron_d2_jaxref_r4_eb89b5'

def setup_inputs(seed: int=0):
    np.random.seed(seed)
    _w = jnp.asarray

    def _L0_attn_setup():
        import jax, jax.numpy as jnp
        import numpy as np
        B, T, D = (4, 512, 256)
        DIN = 2 * D
        SIGN = jnp.array([1.0, -1.0, -1.0, -1.0, -1.0, -1.0, -1.0, -1.0], dtype=jnp.float32)

        def _ln(v, w, b, eps=1e-05):
            m = v.mean(-1, keepdims=True)
            va = ((v - m) ** 2).mean(-1, keepdims=True)
            return (v - m) / jnp.sqrt(va + eps) * w + b

        def _reference_tuple_inner(x, W_in, b_in, basis_real, basis_imag, ln_w, ln_b, theta, omega, sigma, W_sp, b_sp, W_g, b_g, W_out, b_out, norm_w, norm_b):
            x_inner = x @ W_in + b_in
            wr = x_inner @ basis_real
            wi = x_inner @ basis_imag
            vec = _ln(jnp.concatenate([wr, wi], -1), ln_w, ln_b)
            wr, wi = (vec[..., :8], vec[..., 8:])
            cos_t, sin_t = (jnp.cos(theta), jnp.sin(theta))
            scale = jnp.clip(sigma, 0.5, 2.0) * (1.0 + 0.1 * omega)

            def step(carry, w):
                hr, hi = carry
                cr, ci = w
                rr = (hr * cos_t - hi * sin_t) * scale
                ri = (hr * sin_t + hi * cos_t) * scale
                a, b_ = (rr[:, :4], rr[:, 4:])
                ai, bi = (ri[:, :4], ri[:, 4:])
                c, d = (cr[:, :4], cr[:, 4:])
                c2, d2 = (ci[:, :4], ci[:, 4:])
                nr = jnp.concatenate([a * c - d * b_, ai * c2 - d2 * bi], -1)
                ni = jnp.concatenate([d * a + b_ * c, d2 * ai + bi * c2], -1)
                return ((nr, ni), (nr, ni))
            bsz = x.shape[0]
            init = (jnp.zeros((bsz, 8), x.dtype), jnp.zeros((bsz, 8), x.dtype))
            (hr_f, hi_f), (Rs, Is) = jax.lax.scan(step, init, (wr.transpose(1, 0, 2), wi.transpose(1, 0, 2)))
            Rs = Rs.transpose(1, 0, 2)
            Is = Is.transpose(1, 0, 2)
            inv = SIGN * (Rs ** 2 + Is ** 2)
            y = inv @ W_sp + b_sp
            g = jax.nn.silu(x_inner @ W_g + b_g)
            out = y * g @ W_out + b_out
            out = _ln(x + out, norm_w, norm_b)
            final_state = jnp.concatenate([hr_f, hi_f], -1)
            return (out, final_state)
        key = jax.random.key(seed)
        ks = jax.random.split(key, 18)
        s = 1.0 / np.sqrt(D)
        si = 1.0 / np.sqrt(DIN)
        return {'x': jax.random.normal(ks[0], (B, T, D), jnp.float32), 'W_in': jax.random.normal(ks[1], (D, DIN), jnp.float32) * s, 'b_in': jnp.zeros((DIN,), jnp.float32), 'basis_real': jax.random.normal(ks[2], (DIN, 8), jnp.float32) * si, 'basis_imag': jax.random.normal(ks[3], (DIN, 8), jnp.float32) * si, 'ln_w': jnp.ones((16,), jnp.float32), 'ln_b': jnp.zeros((16,), jnp.float32), 'theta': jax.random.normal(ks[4], (8,), jnp.float32) * 0.1, 'omega': jax.random.normal(ks[5], (8,), jnp.float32) * 0.1, 'sigma': jnp.ones((8,), jnp.float32), 'W_sp': jax.random.normal(ks[6], (8, DIN), jnp.float32) * (1.0 / np.sqrt(8)), 'b_sp': jnp.zeros((DIN,), jnp.float32), 'W_g': jax.random.normal(ks[7], (DIN, DIN), jnp.float32) * si, 'b_g': jnp.zeros((DIN,), jnp.float32), 'W_out': jax.random.normal(ks[8], (DIN, D), jnp.float32) * si, 'b_out': jnp.zeros((D,), jnp.float32), 'norm_w': jnp.ones((D,), jnp.float32), 'norm_b': jnp.zeros((D,), jnp.float32)}
    _L0_attn_in = _L0_attn_setup()

    def _L0_ffn_setup():
        import jax, jax.numpy as jnp
        import numpy as np
        CAPACITY_FACTOR = 1.25
        key = jax.random.key(seed)
        ks = jax.random.split(key, 6)
        B, S, H, E = (4, 1024, 256, 8)
        scale = 1.0 / np.sqrt(H)
        return {'tokens': jax.random.normal(ks[0], (B, S, H), dtype=jnp.float32), 'gate_w': jax.random.normal(ks[1], (E, H), dtype=jnp.float32) * scale, 'w1': jax.random.normal(ks[2], (E, H, H), dtype=jnp.float32) * scale, 'b1': jax.random.normal(ks[3], (E, H), dtype=jnp.float32) * 0.01, 'w2': jax.random.normal(ks[4], (E, H, H), dtype=jnp.float32) * scale, 'b2': jax.random.normal(ks[5], (E, H), dtype=jnp.float32) * 0.01}
    _L0_ffn_in = _L0_ffn_setup()

    def _L1_attn_setup():
        import jax, jax.numpy as jnp
        import numpy as np
        D_MODEL = 256
        NUM_HEADS = 16
        HEAD_DIM = D_MODEL // NUM_HEADS
        THETA = 10000.0
        B, S = (2, 512)

        def _apply_rope(t, cos, sin):
            te = t[..., 0::2]
            to = t[..., 1::2]
            re = te * cos - to * sin
            ro = te * sin + to * cos
            out = jnp.stack([re, ro], axis=-1)
            return out.reshape(t.shape)
        key = jax.random.key(seed)
        kx, kq, kk, kv, ko = jax.random.split(key, 5)
        std = 2.0 / (2 * D_MODEL) ** 0.5

        def w(k):
            return jnp.clip(std * jax.random.normal(k, (D_MODEL, D_MODEL), jnp.float32), -3.0 * std, 3.0 * std)
        return {'x': jax.random.normal(kx, (B, S, D_MODEL), jnp.float32), 'Wq': w(kq), 'Wk': w(kk), 'Wv': w(kv), 'Wo': w(ko)}
    _L1_attn_in = _L1_attn_setup()

    def _L1_ffn_setup():
        import jax, jax.numpy as jnp
        import numpy as np
        D_MODEL = 256
        D_OUT = 256
        RANK = 16
        NUM_TRUE = 8
        NUM_NULL = 2
        TOP_K = 2
        SCALING = 32.0 / 16.0
        key = jax.random.key(seed)
        ks = jax.random.split(key, 6)
        x = jax.random.normal(ks[0], (4, 1024, D_MODEL), dtype=jnp.float32)
        base_w = jax.random.normal(ks[1], (D_OUT, D_MODEL), dtype=jnp.float32) / np.sqrt(D_MODEL)
        base_b = jax.random.normal(ks[2], (D_OUT,), dtype=jnp.float32) * 0.01
        gate_w = jax.random.normal(ks[3], (NUM_TRUE + NUM_NULL, D_MODEL), dtype=jnp.float32) / np.sqrt(D_MODEL)
        lora_A = jax.random.normal(ks[4], (NUM_TRUE, RANK, D_MODEL), dtype=jnp.float32) / np.sqrt(D_MODEL)
        lora_B = jax.random.normal(ks[5], (NUM_TRUE, D_OUT, RANK), dtype=jnp.float32) * 0.01
        return {'x': x, 'base_w': base_w, 'base_b': base_b, 'gate_w': gate_w, 'lora_A': lora_A, 'lora_B': lora_B}
    _L1_ffn_in = _L1_ffn_setup()
    _d = {'L0_attn_x': _L0_attn_in['x'], 'L0_attn_W_in': _L0_attn_in['W_in'], 'L0_attn_b_in': _L0_attn_in['b_in'], 'L0_attn_basis_real': _L0_attn_in['basis_real'], 'L0_attn_basis_imag': _L0_attn_in['basis_imag'], 'L0_attn_ln_w': _L0_attn_in['ln_w'], 'L0_attn_ln_b': _L0_attn_in['ln_b'], 'L0_attn_theta': _L0_attn_in['theta'], 'L0_attn_omega': _L0_attn_in['omega'], 'L0_attn_sigma': _L0_attn_in['sigma'], 'L0_attn_W_sp': _L0_attn_in['W_sp'], 'L0_attn_b_sp': _L0_attn_in['b_sp'], 'L0_attn_W_g': _L0_attn_in['W_g'], 'L0_attn_b_g': _L0_attn_in['b_g'], 'L0_attn_W_out': _L0_attn_in['W_out'], 'L0_attn_b_out': _L0_attn_in['b_out'], 'L0_attn_norm_w': _L0_attn_in['norm_w'], 'L0_attn_norm_b': _L0_attn_in['norm_b'], 'L0_ffn_gate_w': _L0_ffn_in['gate_w'], 'L0_ffn_w1': _L0_ffn_in['w1'], 'L0_ffn_b1': _L0_ffn_in['b1'], 'L0_ffn_w2': _L0_ffn_in['w2'], 'L0_ffn_b2': _L0_ffn_in['b2'], 'L1_attn_Wq': _L1_attn_in['Wq'], 'L1_attn_Wk': _L1_attn_in['Wk'], 'L1_attn_Wv': _L1_attn_in['Wv'], 'L1_attn_Wo': _L1_attn_in['Wo'], 'L1_ffn_base_w': _L1_ffn_in['base_w'], 'L1_ffn_base_b': _L1_ffn_in['base_b'], 'L1_ffn_gate_w': _L1_ffn_in['gate_w'], 'L1_ffn_lora_A': _L1_ffn_in['lora_A'], 'L1_ffn_lora_B': _L1_ffn_in['lora_B']}
    _x0 = _d['L0_attn_x']
    _d['L0_attn_x'] = jax.random.normal(jax.random.fold_in(jax.random.key(seed), 1), (16, 1024, 256), dtype=_x0.dtype)
    del _x0
    return _d

def reference(L0_attn_x, L0_attn_W_in, L0_attn_b_in, L0_attn_basis_real, L0_attn_basis_imag, L0_attn_ln_w, L0_attn_ln_b, L0_attn_theta, L0_attn_omega, L0_attn_sigma, L0_attn_W_sp, L0_attn_b_sp, L0_attn_W_g, L0_attn_b_g, L0_attn_W_out, L0_attn_b_out, L0_attn_norm_w, L0_attn_norm_b, L0_ffn_gate_w, L0_ffn_w1, L0_ffn_b1, L0_ffn_w2, L0_ffn_b2, L1_attn_Wq, L1_attn_Wk, L1_attn_Wv, L1_attn_Wo, L1_ffn_base_w, L1_ffn_base_b, L1_ffn_gate_w, L1_ffn_lora_A, L1_ffn_lora_B):

    def _L0_attn_ref(x, W_in, b_in, basis_real, basis_imag, ln_w, ln_b, theta, omega, sigma, W_sp, b_sp, W_g, b_g, W_out, b_out, norm_w, norm_b):
        import jax, jax.numpy as jnp
        import numpy as np
        B, T, D = (4, 512, 256)
        DIN = 2 * D
        SIGN = jnp.array([1.0, -1.0, -1.0, -1.0, -1.0, -1.0, -1.0, -1.0], dtype=jnp.float32)

        def _ln(v, w, b, eps=1e-05):
            m = v.mean(-1, keepdims=True)
            va = ((v - m) ** 2).mean(-1, keepdims=True)
            return (v - m) / jnp.sqrt(va + eps) * w + b

        def _reference_tuple_inner(x, W_in, b_in, basis_real, basis_imag, ln_w, ln_b, theta, omega, sigma, W_sp, b_sp, W_g, b_g, W_out, b_out, norm_w, norm_b):
            x_inner = x @ W_in + b_in
            wr = x_inner @ basis_real
            wi = x_inner @ basis_imag
            vec = _ln(jnp.concatenate([wr, wi], -1), ln_w, ln_b)
            wr, wi = (vec[..., :8], vec[..., 8:])
            cos_t, sin_t = (jnp.cos(theta), jnp.sin(theta))
            scale = jnp.clip(sigma, 0.5, 2.0) * (1.0 + 0.1 * omega)

            def step(carry, w):
                hr, hi = carry
                cr, ci = w
                rr = (hr * cos_t - hi * sin_t) * scale
                ri = (hr * sin_t + hi * cos_t) * scale
                a, b_ = (rr[:, :4], rr[:, 4:])
                ai, bi = (ri[:, :4], ri[:, 4:])
                c, d = (cr[:, :4], cr[:, 4:])
                c2, d2 = (ci[:, :4], ci[:, 4:])
                nr = jnp.concatenate([a * c - d * b_, ai * c2 - d2 * bi], -1)
                ni = jnp.concatenate([d * a + b_ * c, d2 * ai + bi * c2], -1)
                return ((nr, ni), (nr, ni))
            bsz = x.shape[0]
            init = (jnp.zeros((bsz, 8), x.dtype), jnp.zeros((bsz, 8), x.dtype))
            (hr_f, hi_f), (Rs, Is) = jax.lax.scan(step, init, (wr.transpose(1, 0, 2), wi.transpose(1, 0, 2)))
            Rs = Rs.transpose(1, 0, 2)
            Is = Is.transpose(1, 0, 2)
            inv = SIGN * (Rs ** 2 + Is ** 2)
            y = inv @ W_sp + b_sp
            g = jax.nn.silu(x_inner @ W_g + b_g)
            out = y * g @ W_out + b_out
            out = _ln(x + out, norm_w, norm_b)
            final_state = jnp.concatenate([hr_f, hi_f], -1)
            return (out, final_state)
        return _reference_tuple_inner(x, W_in, b_in, basis_real, basis_imag, ln_w, ln_b, theta, omega, sigma, W_sp, b_sp, W_g, b_g, W_out, b_out, norm_w, norm_b)[0]

    def _L0_ffn_ref(tokens, gate_w, w1, b1, w2, b2):
        import jax, jax.numpy as jnp
        import numpy as np
        CAPACITY_FACTOR = 1.25
        B, S, H = tokens.shape
        E = gate_w.shape[0]
        N = B * S
        cap = int(CAPACITY_FACTOR * N / E)
        x = tokens.reshape(N, H)
        probs = jax.nn.softmax(x @ gate_w.T, axis=-1)
        top2_w, top2_idx = jax.lax.top_k(probs, 2)
        a_e = top2_idx.reshape(-1)
        a_w = top2_w.reshape(-1)
        tok_id = jnp.arange(2 * N) // 2
        counts = jnp.bincount(a_e, length=E)
        keep = counts <= cap
        valid = keep[a_e]
        onehot = jax.nn.one_hot(a_e, E, dtype=jnp.int32)
        pos = jnp.take_along_axis(jnp.cumsum(onehot, axis=0) - 1, a_e[:, None], axis=1)[:, 0]
        p = jnp.where(valid, jnp.minimum(pos, cap - 1), cap)
        x_a = x[tok_id]
        buf = jnp.zeros((E, cap + 1, H), dtype=x.dtype).at[a_e, p].set(x_a)
        h = jax.nn.silu(jnp.einsum('ech,efh->ecf', buf, w1) + b1[:, None, :])
        y = jnp.einsum('ecf,egf->ecg', h, w2) + b2[:, None, :]
        contrib = y[a_e, p] * (a_w * valid.astype(x.dtype))[:, None]
        out = contrib.reshape(N, 2, H).sum(axis=1)
        return out.reshape(B, S, H)

    def _L1_attn_ref(x, Wq, Wk, Wv, Wo):
        import jax, jax.numpy as jnp
        import numpy as np
        D_MODEL = 256
        NUM_HEADS = 16
        HEAD_DIM = D_MODEL // NUM_HEADS
        THETA = 10000.0
        B, S = (2, 512)

        def _apply_rope(t, cos, sin):
            te = t[..., 0::2]
            to = t[..., 1::2]
            re = te * cos - to * sin
            ro = te * sin + to * cos
            out = jnp.stack([re, ro], axis=-1)
            return out.reshape(t.shape)
        Bv, Sv, _ = x.shape

        def proj(W):
            return jnp.einsum('bsd,ed->bse', x, W).reshape(Bv, Sv, NUM_HEADS, HEAD_DIM).transpose(0, 2, 1, 3)
        q, k, v = (proj(Wq), proj(Wk), proj(Wv))
        pos = jnp.arange(Sv, dtype=jnp.float32)
        inv_freq = THETA ** (-jnp.arange(0, HEAD_DIM, 2, dtype=jnp.float32) / HEAD_DIM)
        ang = pos[:, None] * inv_freq[None, :]
        cos, sin = (jnp.cos(ang), jnp.sin(ang))
        q = _apply_rope(q, cos, sin)
        k = _apply_rope(k, cos, sin)
        scale = 1.0 / jnp.sqrt(jnp.float32(HEAD_DIM))
        scores = jnp.einsum('bhqd,bhkd->bhqk', q.astype(jnp.float32), k.astype(jnp.float32)) * scale
        causal = jnp.tril(jnp.ones((Sv, Sv), dtype=bool))
        scores = jnp.where(causal[None, None], scores, -jnp.inf)
        attn = jax.nn.softmax(scores, axis=-1)
        out = jnp.einsum('bhqk,bhkd->bhqd', attn, v.astype(jnp.float32))
        out = out.transpose(0, 2, 1, 3).reshape(Bv, Sv, D_MODEL)
        return jnp.einsum('bsd,ed->bse', out, Wo)

    def _L1_ffn_ref(x, base_w, base_b, gate_w, lora_A, lora_B):
        import jax, jax.numpy as jnp
        import numpy as np
        D_MODEL = 256
        D_OUT = 256
        RANK = 16
        NUM_TRUE = 8
        NUM_NULL = 2
        TOP_K = 2
        SCALING = 32.0 / 16.0
        xf = x.reshape(-1, x.shape[-1])
        logits = jnp.einsum('td,ed->te', xf, gate_w)
        probs = jax.nn.softmax(logits, axis=-1)
        weights, selected = jax.lax.top_k(probs, TOP_K)
        true_mask = (selected < NUM_TRUE).astype(weights.dtype)
        tw = weights * true_mask
        denom = tw.sum(axis=-1, keepdims=True)
        denom = jnp.where(denom > 0, denom, jnp.ones_like(denom))
        nw = tw / denom
        onehot = jax.nn.one_hot(selected, NUM_TRUE, dtype=nw.dtype)
        ew = jnp.einsum('tk,tke->te', nw, onehot)
        z = jnp.einsum('td,erd->ter', xf, lora_A)
        moe = jnp.einsum('ter,te,eor->to', z, ew, lora_B) * SCALING
        base = jnp.einsum('td,od->to', xf, base_w) + base_b
        out = (base + moe).reshape(x.shape[:-1] + (D_OUT,))
        return out
    x = L0_attn_x
    x = x + 0.5 * _L0_ffn_ref(_layernorm(x, axis=-1), L0_ffn_gate_w, L0_ffn_w1, L0_ffn_b1, L0_ffn_w2, L0_ffn_b2)
    x = x + _L0_attn_ref(_layernorm(x, axis=-1), L0_attn_W_in, L0_attn_b_in, L0_attn_basis_real, L0_attn_basis_imag, L0_attn_ln_w, L0_attn_ln_b, L0_attn_theta, L0_attn_omega, L0_attn_sigma, L0_attn_W_sp, L0_attn_b_sp, L0_attn_W_g, L0_attn_b_g, L0_attn_W_out, L0_attn_b_out, L0_attn_norm_w, L0_attn_norm_b)
    x = x + 0.5 * _L0_ffn_ref(_layernorm(x, axis=-1), L0_ffn_gate_w, L0_ffn_w1, L0_ffn_b1, L0_ffn_w2, L0_ffn_b2)
    x = x + 0.5 * _L1_ffn_ref(_layernorm(x, axis=-1), L1_ffn_base_w, L1_ffn_base_b, L1_ffn_gate_w, L1_ffn_lora_A, L1_ffn_lora_B)
    x = x + _L1_attn_ref(_layernorm(x, axis=-1), L1_attn_Wq, L1_attn_Wk, L1_attn_Wv, L1_attn_Wo)
    x = x + 0.5 * _L1_ffn_ref(_layernorm(x, axis=-1), L1_ffn_base_w, L1_ffn_base_b, L1_ffn_gate_w, L1_ffn_lora_A, L1_ffn_lora_B)
    return x

_drawn_inputs = setup_inputs


def setup_inputs(seed=0):
    import zlib

    import numpy as np

    out = dict(_drawn_inputs(seed))
    spreads = {'L0_attn_b_in': (0.0, 0.8),
     'L0_attn_ln_w': (1.0, 0.2),
     'L0_attn_ln_b': (0.0, 0.1),
     'L0_attn_sigma': (1.0, 0.2),
     'L0_attn_b_sp': (0.0, 0.1),
     'L0_attn_b_g': (0.0, 0.8),
     'L0_attn_b_out': (0.0, 0.1),
     'L0_attn_norm_w': (1.0, 0.2),
     'L0_attn_norm_b': (0.0, 0.1)}
    factors = {'L1_ffn_base_b': 8.0}
    for name, (base, spread) in spreads.items():
        noise = np.random.default_rng([zlib.crc32(name.encode()), seed]).standard_normal(out[name].shape)
        drawn = base * np.exp(spread * noise) if base else spread * noise
        out[name] = jnp.asarray(drawn.astype(out[name].dtype))
    for name, factor in factors.items():
        out[name] = (out[name] * factor).astype(out[name].dtype)
    return out
```

```python
from contextlib import ExitStack, contextmanager

import concourse.bass as bass
from concourse import mybir

F32 = mybir.dt.float32
BF16 = mybir.dt.bfloat16
U32 = mybir.dt.uint32
I32 = mybir.dt.int32
ACT = mybir.ActivationFunctionType
ALU = mybir.AluOpType
AX = mybir.AxisListType

P = 128
D = 256
DC = D // P
S = 1024
TS = S // P
DIN = 512
FC = DIN // P
E0 = 8
E1 = 10
NT = 8
RANK = 16
NZ = NT * RANK
NZG = NZ + E1
H = 16
HD = 16
HG = 4
NHG = H // HG
QC = 512
NQC = S // QC
KQ = QC // P
GT = 4
GTOK = GT * P
EPS = 1e-5
MASKED = -1e30
D_LIMIT = 1e30
INV_D_LIMIT = 1e25
SLOTS = 6
QPARTS = [0, 0, 0, 1, 1, 2]
KPARTS = [0, 1, 2, 0, 1, 0]
ROWS = SLOTS * HD
RUNS = (((0, 0, 1), (1, 0, 1), (2, 0, 2), (4, 1, 2)), ((0, 0, 3), (3, 0, 2), (5, 0, 1)))
VW = HD + 1
STEPS = NHG * sum(KQ * (qc + 1) for qc in range(NQC))


def at(buf, k):
    if isinstance(k, int):
        return buf[:, k]
    return buf[:, bass.ds(k, 1)].squeeze(1)


def row_bcast(ap, n, shape):
    return ap.unsqueeze(1).to_broadcast(shape)


class Pools:

    def __init__(self, nc, ctx, prefix):
        self.nc, self.ctx, self.prefix, self.sems = nc, ctx, prefix, []

    def sb(self, name, shape, dt=F32):
        return self.ctx.enter_context(self.nc.sbuf_tensor(self.prefix + name, shape, dt))

    def ps(self, name, shape, dt=F32):
        return self.ctx.enter_context(self.nc.psum_tensor(self.prefix + name, shape, dt))

    def sem(self, name):
        self.sems.append(self.nc.alloc_semaphore(self.prefix + name))
        return self.sems[-1]

    def free_sems(self):
        self.nc.all_engine_barrier()
        self.nc.clear_and_free_semaphores(self.sems)
        self.nc.all_engine_barrier()


@contextmanager
def only_if(eng, flag):
    if flag is None:
        yield
    else:
        value = eng.value_load(flag, min_val=0, max_val=1)
        with eng.If(value == 1):
            yield
        with eng.Else():
            eng.nop()
        eng.nop()


def norm_stats(dve, rows, stats, moments):
    for t in range(GT):
        dve.bn_stats(stats[:, t, :], rows(t))
    dve.drain()
    for t in range(GT):
        last = dve.bn_aggr(moments[:, t, :], stats[:, t, :])
    return last


def norm_rstd(pool, moments, var_eps, rstd, eps, minus_half):
    pool.tensor_tensor(var_eps, moments[:, :, 1], eps, ALU.add)
    pool.drain()
    return pool.tensor_tensor(rstd, var_eps, minus_half, ALU.pow)


def norm_apply(dve, out, rows, moments, rstd):
    for t in range(GT):
        last = dve.tensor_scalar(out[:, t, :], rows(t), moments[:, t, 0:1], rstd[:, t:t + 1], ALU.subtract, ALU.mult)
    return last


def token_pass(nc, io, const, stage, mix, src, fallback, dst):
    n_groups = io["tokens"] // GTOK
    pre = f"t{stage}_"
    with ExitStack() as ctx:
        m = Pools(nc, ctx, pre)
        x = m.sb("x", [P, 4, GT, D])
        xn = m.sb("xn", [P, GT, D])
        xnT = m.sb("xnT", [P, DC, GTOK])
        stats, moments = m.sb("stats", [P, GT, 6]), m.sb("moments", [P, GT, 2])
        var_eps, rstd = m.sb("var_eps", [P, GT]), m.sb("rstd", [P, GT])
        gate = m.sb("gate", [P, DC, E0])
        logT = m.sb("logT", [E0, GTOK])
        logits = m.sb("logits", [P, GT, E0])
        best = m.sb("best", [P, GT, 8])
        best_at = m.sb("best_at", [P, GT, 8], U32)
        chosen0, chosen1 = m.sb("chosen0", [P, GT, E0]), m.sb("chosen1", [P, GT, E0])
        tally = m.sb("tally", [P, GT, E0])
        tally_p = m.sb("tally_p", [P, E0])
        any_keep = m.sb("any_keep", [P, 1])
        psT = [m.ps(f"psT{c}", [P, GTOK]) for c in range(DC)]
        ps_logT = m.ps("ps_logT", [P, GTOK])
        ps_log = m.ps("ps_log", [P, 512])

        loaded, weights = m.sem("loaded"), m.sem("weights")
        moments_ready, rstd_ready = m.sem("moments_ready"), m.sem("rstd_ready")
        xn_ready, turned, xnT_ready = m.sem("xn_ready"), m.sem("turned"), m.sem("xnT_ready")
        logT_ready, logT_copied = m.sem("logT_ready"), m.sem("logT_copied")
        log_ready, group_done, log_waited = m.sem("log_ready"), m.sem("group_done"), m.sem("log_waited")
        tally_ready, summed, flagged = m.sem("tally_ready"), m.sem("summed"), m.sem("flagged")
        if mix:
            w_inT, w_g = m.sb("w_inT", [P, FC, D]), m.sb("w_g", [P, FC, DIN])
            b_in, b_g, b_sp = m.sb("b_in", [P, FC]), m.sb("b_g", [P, FC]), m.sb("b_sp", [P, FC])
            w_out = m.sb("w_out", [P, FC, D])
            b_out, norm_w, norm_b = m.sb("b_out", [P, D]), m.sb("norm_w", [P, D]), m.sb("norm_b", [P, D])
            w_ig, b_ig, w_so = m.sb("w_ig", [P, DC, DIN]), m.sb("b_ig", [P, FC]), m.sb("w_so", [P, FC, D])
            xn_b, x_b = m.sb("xn_b", [P, 2, GT, D]), m.sb("x_b", [P, 2, GT, D])
            silu = m.sb("silu", [P, FC, GTOK])
            r = m.sb("r", [P, GT, D])
            xn3, xn3T = m.sb("xn3", [P, GT, D]), m.sb("xn3T", [P, DC, GTOK])
            stats2, moments2 = m.sb("stats2", [P, GT, 6]), m.sb("moments2", [P, GT, 2])
            stats3, moments3 = m.sb("stats3", [P, GT, 6]), m.sb("moments3", [P, GT, 2])
            var_eps2, rstd2 = m.sb("var_eps2", [P, GT]), m.sb("rstd2", [P, GT])
            var_eps3, rstd3 = m.sb("var_eps3", [P, GT]), m.sb("rstd3", [P, GT])
            psG = [m.ps(f"psG{k}", [P, GTOK]) for k in range(2)]
            psY = [m.ps(f"psY{k}", [P, 2, D]) for k in range(2)]
            folded_pe, folded = m.sem("folded_pe"), m.sem("folded")
            shifted_ready, gate_ready, gate_silu = m.sem("shifted_ready"), m.sem("gate_ready"), m.sem("gate_silu")
            mixed, r_ready, x_new = m.sem("mixed"), m.sem("r_ready"), m.sem("x_new")
            moments2_ready, rstd2_ready = m.sem("moments2_ready"), m.sem("rstd2_ready")
            moments3_ready, rstd3_ready = m.sem("moments3_ready"), m.sem("rstd3_ready")
            xn3_ready, turned3, xn3T_ready = m.sem("xn3_ready"), m.sem("turned3"), m.sem("xn3T_ready")
            stored, slot_waited = m.sem("stored"), m.sem("slot_waited")
        rT, rT_ready = (xn3T, xn3T_ready) if mix else (xnT, xnT_ready)

        src_g, dst_g, fb_g = (None if a is None else a.rearrange("(g t p) d -> g p t d", t=GT, p=P)
                              for a in (src, dst, fallback))

        def dram_at(v, g):
            return v[g] if isinstance(g, int) else v[bass.ds(g, 1)].squeeze(0)

        ctx.callback(m.free_sems)
        block = ctx.enter_context(nc.Block())

        @block.sync
        def _(sp):
            def load_from(v):
                def load(g):
                    sp.dma_start(at(x, g % 4), dram_at(v, g)).then_inc(loaded, 16)
                return load

            def run(load):
                def slot_done(g):
                    if mix:
                        sp.wait_ge(x_new, g + 1)
                        sp.dma_start(dram_at(dst_g, g), at(x, g % 4)).then_inc(stored, 16)
                        sp.wait_ge(stored, g * 16 + 16)
                        sp.sem_inc(slot_waited, 1)
                    else:
                        sp.wait_ge(xn_ready, g + 1)

                load(0)
                sp.wait_ge(loaded, 16)
                load(1)
                with sp.Fori(0, n_groups - 2) as g:
                    slot_done(g)
                    sp.wait_ge(loaded, g * 16 + 32)
                    load(g + 2)
                slot_done(n_groups - 2)
                slot_done(n_groups - 1)

            sp.dma_start(gate[:], io["gate0T"].rearrange("(c p) e -> p c e", p=P)).then_inc(weights, 16)
            if mix:
                for buf, name in ((w_inT, "w_inT"), (w_g, "w_g"), (w_out, "w_out")):
                    sp.dma_start(buf[:], io[name].rearrange("(c p) e -> p c e", p=P)).then_inc(weights, 16)
                for buf, name in ((b_in, "b_in"), (b_g, "b_g"), (b_sp, "b_sp"), (b_out, "b_out"),
                                  (norm_w, "norm_w"), (norm_b, "norm_b")):
                    sp.dma_start(buf[:], io[name]).then_inc(weights, 16)
            if fallback is None:
                run(load_from(src_g))
            else:
                kept = sp.value_load(const["flag"][0:1, stage - 1:stage], min_val=0, max_val=1)
                with sp.If(kept == 1):
                    run(load_from(fb_g))
                with sp.Else():
                    run(load_from(src_g))
                sp.nop()
            if mix:
                sp.wait_ge(stored, 16 * n_groups)

        n_weights = 16 * (10 if mix else 1)

        @block.tensor
        def _(pe):
            pe.wait_ge(weights, n_weights)
            if mix:
                for c in range(DC):
                    for j in range(FC):
                        last = pe.matmul(psG[c][:], w_inT[:, j, c * P:(c + 1) * P], w_g[:, j, :],
                                         start=(j == 0), stop=(j == FC - 1))
                for f in range(FC):
                    for j in range(FC):
                        last = pe.matmul(ps_log[:, f:f + 1], w_g[:, j, f * P:(f + 1) * P], b_in[:, j:j + 1],
                                         start=(j == 0), stop=(j == FC - 1))
                last.then_inc(folded_pe, 1)
                pe.wait_ge(folded, 4)

            def turn(src_tile, g, ready, done_sem):
                pe.wait_ge(ready, g + 1)
                for c in range(DC):
                    for t in range(GT):
                        last = pe.transpose(psT[c][:, t * P:(t + 1) * P], src_tile[:, t, c * P:(c + 1) * P],
                                            const["ident"][:])
                    last.then_inc(done_sem, 1)

            def log_parts(g):
                pe.wait_ge(rT_ready, (g + 1) * DC)
                for c in range(DC):
                    last = pe.matmul(ps_logT[0:E0, :], gate[:, c, :], rT[:, c, :], start=(c == 0), stop=(c == DC - 1))
                last.then_inc(logT_ready, 1)

            def log_turn(g):
                pe.wait_ge(logT_copied, g + 1)
                pe.wait_ge(group_done, g + 1)
                pe.sem_inc(log_waited, 1)
                for t in range(GT):
                    last = pe.transpose(ps_log[:, t * E0:(t + 1) * E0], logT[:, t * P:(t + 1) * P],
                                        const["ident"][0:E0, 0:E0])
                last.then_inc(log_ready, 1)

            def mix_gate(g):
                pe.wait_ge(xnT_ready, (g + 1) * DC)
                for f in range(FC):
                    pe.wait_ge(gate_silu, g * FC + f + 1)
                    for c in range(DC):
                        last = pe.matmul(psG[f % 2][:], w_ig[:, c, f * P:(f + 1) * P], xnT[:, c, :],
                                         start=(c == 0), stop=(c == DC - 1))
                    last.then_inc(gate_ready, 1)

            def mix_out(g):
                for t in range(GT):
                    if t == 0:
                        pe.wait_ge(gate_silu, (g + 1) * FC + 2)
                    if t % 2 == 0:
                        pe.wait_ge(r_ready, g * 2 + t // 2 + 1)
                    for f in range(FC):
                        last = pe.matmul(psY[t // 2][:, t % 2, :], silu[:, f, t * P:(t + 1) * P], w_so[:, f, :],
                                         start=(f == 0), stop=(f == FC - 1))
                    if t % 2:
                        last.then_inc(mixed, 1)

            if not mix:
                with pe.Fori(0, n_groups) as g:
                    turn(xn, g, xn_ready, turned)
                    log_parts(g)
                    log_turn(g)
            else:
                turn(xn, 0, xn_ready, turned)
                mix_gate(0)
                mix_out(0)
                with pe.Fori(1, n_groups) as g:
                    turn(xn, g, xn_ready, turned)
                    mix_gate(g)
                    mix_out(g)
                    turn(xn3, g - 1, xn3_ready, turned3)
                    log_parts(g - 1)
                    log_turn(g - 1)
                turn(xn3, n_groups - 1, xn3_ready, turned3)
                log_parts(n_groups - 1)
                log_turn(n_groups - 1)
            pe.wait_ge(tally_ready, 1)
            pe.matmul(ps_logT[:, 0:E0], const["ones"][:], tally_p[:], start=True, stop=True).then_inc(summed, 1)

        @block.scalar
        def _(act):
            if mix:
                act.wait_ge(folded_pe, 1)
                for c in range(DC):
                    act.activation(w_ig[:, c, :], psG[c][:], ACT.Copy).then_inc(folded, 1)

            def copy_turned(g, done_sem, out, out_ready):
                for c in range(DC):
                    act.wait_ge(done_sem, g * DC + c + 1)
                    act.activation(out[:, c, :], psT[c][:], ACT.Copy).then_inc(out_ready, 1)

            def copy_logT(g):
                act.wait_ge(logT_ready, g + 1)
                act.activation(logT[:], ps_logT[0:E0, :], ACT.Copy).then_inc(logT_copied, 1)

            def silus(g):
                for f in range(FC):
                    act.wait_ge(gate_ready, g * FC + f + 1)
                    act.activation(silu[:, f, :], psG[f % 2][:], ACT.Silu, bias=b_ig[:, f:f + 1]).then_inc(gate_silu, 1)

            if not mix:
                with act.Fori(0, n_groups) as g:
                    copy_turned(g, turned, xnT, xnT_ready)
                    copy_logT(g)
            else:
                act.sem_inc(gate_silu, 2)
                act.wait_ge(folded, 4)
                copy_turned(0, turned, xnT, xnT_ready)
                silus(0)
                with act.Fori(1, n_groups) as g:
                    copy_turned(g, turned, xnT, xnT_ready)
                    silus(g)
                    copy_turned(g - 1, turned3, xn3T, xn3T_ready)
                    copy_logT(g - 1)
                copy_turned(n_groups - 1, turned3, xn3T, xn3T_ready)
                copy_logT(n_groups - 1)

        @block.gpsimd
        def _(pool):
            def rstd_of(g, ready, mom, ve, rs, done_sem):
                pool.wait_ge(ready, g + 1)
                norm_rstd(pool, mom, ve[:], rs[:], const["eps"][:], const["minus_half"][:]).then_inc(done_sem, 1)

            def shifted(g):
                pool.wait_ge(xn_ready, g + 1)
                pool.tensor_tensor(at(xn_b, g % 2), xn[:], row_bcast(b_out[:], GT, [P, GT, D]), ALU.add)
                pool.tensor_tensor(at(x_b, g % 2), at(x, g % 4), row_bcast(norm_b[:], GT, [P, GT, D]),
                                   ALU.add).then_inc(shifted_ready, 1)

            if not mix:
                with pool.Fori(0, n_groups) as g:
                    rstd_of(g, moments_ready, moments, var_eps, rstd, rstd_ready)
            else:
                pool.wait_ge(weights, n_weights)
                rstd_of(0, moments_ready, moments, var_eps, rstd, rstd_ready)
                shifted(0)
                with pool.Fori(1, n_groups) as g:
                    rstd_of(g, moments_ready, moments, var_eps, rstd, rstd_ready)
                    shifted(g)
                    rstd_of(g - 1, moments2_ready, moments2, var_eps2, rstd2, rstd2_ready)
                    rstd_of(g - 1, moments3_ready, moments3, var_eps3, rstd3, rstd3_ready)
                rstd_of(n_groups - 1, moments2_ready, moments2, var_eps2, rstd2, rstd2_ready)
                rstd_of(n_groups - 1, moments3_ready, moments3, var_eps3, rstd3, rstd3_ready)

        @block.vector
        def _(dve):
            if mix:
                dve.wait_ge(weights, n_weights)
                for f in range(FC):
                    last = dve.tensor_scalar(w_so[:, f, :], w_out[:, f, :], b_sp[:, f:f + 1], None, ALU.mult)
                last.then_inc(folded, 1)
                dve.wait_ge(folded_pe, 1)
                dve.tensor_tensor(b_ig[:], ps_log[:, 0:FC], b_g[:], ALU.add).then_inc(folded, 1)
                dve.sem_inc(r_ready, 2)
            dve.memset(tally[:], 0.0)
            dve.sem_inc(group_done, 1)

            def normalise(g):
                dve.wait_ge(loaded, g * 16 + 16)
                rows = lambda t: at(x, g % 4)[:, t, :]
                norm_stats(dve, rows, stats, moments).then_inc(moments_ready, 1)
                dve.wait_ge(rstd_ready, g + 1)
                if not isinstance(g, int) or g > 0:
                    dve.wait_ge(turned, g * DC)
                    if mix:
                        dve.wait_ge(shifted_ready, g)
                norm_apply(dve, xn, rows, moments, rstd).then_inc(xn_ready, 1)

            def mix_sums(g):
                dve.wait_ge(shifted_ready, g + 1)
                for u in range(GT // 2):
                    dve.wait_ge(mixed, g * 2 + u + 1)
                    dve.tensor_tensor(r[:, 2 * u:2 * u + 2, :], psY[u][:], at(xn_b, g % 2)[:, 2 * u:2 * u + 2, :],
                                      ALU.add).then_inc(r_ready, 1)
                dve.drain()
                norm_stats(dve, lambda t: r[:, t, :], stats2, moments2).then_inc(moments2_ready, 1)
                dve.wait_ge(rstd2_ready, g + 1)
                for t in range(GT):
                    dve.tensor_scalar(r[:, t, :], r[:, t, :], moments2[:, t, 0:1], rstd2[:, t:t + 1],
                                      ALU.subtract, ALU.mult)
                dve.drain()
                dve.tensor_tensor(r[:], r[:], row_bcast(norm_w[:], GT, [P, GT, D]), ALU.mult)
                dve.drain()
                dve.tensor_tensor(at(x, g % 4), r[:], at(x_b, g % 2), ALU.add).then_inc(x_new, 1)
                dve.drain()
                rows = lambda t: at(x, g % 4)[:, t, :]
                norm_stats(dve, rows, stats3, moments3).then_inc(moments3_ready, 1)
                dve.wait_ge(rstd3_ready, g + 1)
                norm_apply(dve, xn3, rows, moments3, rstd3).then_inc(xn3_ready, 1)

            def route(g):
                dve.wait_ge(log_ready, g + 1)
                dve.tensor_copy(logits[:], ps_log[:, 0:GT * E0]).then_inc(group_done, 1)
                dve.drain()
                for t in range(GT):
                    dve.max(best[:, t, :], logits[:, t, :])
                dve.drain()
                for t in range(GT):
                    dve.max_index(best_at[:, t, :], best[:, t, :], logits[:, t, :])
                dve.drain()
                for k, chosen in ((0, chosen0), (1, chosen1)):
                    dve.tensor_tensor(chosen[:], const["iota0"][:], best_at[:, :, k:k + 1].to_broadcast([P, GT, E0]),
                                      ALU.is_equal)
                dve.drain()
                dve.tensor_tensor(tally[:], tally[:], chosen0[:], ALU.add)
                dve.drain()
                dve.tensor_tensor(tally[:], tally[:], chosen1[:], ALU.add)

            if not mix:
                normalise(0)
                with dve.Fori(1, n_groups) as g:
                    normalise(g)
                    route(g - 1)
                route(n_groups - 1)
            else:
                normalise(0)
                with dve.Fori(1, n_groups) as g:
                    normalise(g)
                    mix_sums(g - 1)
                    route(g - 1)
                mix_sums(n_groups - 1)
                route(n_groups - 1)
            dve.drain()
            dve.tensor_reduce(tally_p[:], tally[:].rearrange("p t e -> p e t"), AX.X, ALU.add).then_inc(tally_ready, 1)
            dve.wait_ge(summed, 1)
            keep = const["keep"][:, stage, :]
            dve.tensor_scalar(keep, ps_logT[:, 0:E0], float(io["cap"]), None, ALU.is_le)
            dve.drain()
            dve.tensor_reduce(any_keep[:], keep, AX.X, ALU.max)
            dve.drain()
            dve.tensor_copy(const["flag"][:, stage:stage + 1], any_keep[:])



def moe_pass(nc, io, const, stage, src, dst):
    n_groups = io["tokens"] // GTOK
    with ExitStack() as ctx:
        m = Pools(nc, ctx, f"e{stage}_")
        x, xn, xnT = m.sb("x", [P, GT, D]), m.sb("xn", [P, GT, D]), m.sb("xnT", [P, DC, GTOK])
        stats, moments = m.sb("stats", [P, GT, 6]), m.sb("moments", [P, GT, 2])
        var_eps, rstd = m.sb("var_eps", [P, GT]), m.sb("rstd", [P, GT])
        gate = m.sb("gate", [P, DC, E0])
        w1, w2 = m.sb("w1", [P, E0, DC, D]), m.sb("w2", [P, E0, DC, D])
        b1, b2 = m.sb("b1", [P, E0, DC]), m.sb("b2", [P, E0, D])
        logits, share = m.sb("logits", [P, GT, E0]), m.sb("share", [P, GT, E0])
        best, best_at = m.sb("best", [P, GT, 8]), m.sb("best_at", [P, GT, 8], U32)
        chosen0, chosen1 = m.sb("chosen0", [P, GT, E0]), m.sb("chosen1", [P, GT, E0])
        total, inv_total = m.sb("total", [P, GT]), m.sb("inv_total", [P, GT])
        hidden, y = m.sb("hidden", [P, DC, GTOK]), m.sb("y", [P, 2, D])
        psT = [m.ps(f"psT{c}", [P, GTOK]) for c in range(DC)]
        psH = [m.ps(f"psH{c}", [P, GTOK]) for c in range(DC)]
        psY = [m.ps(f"psY{u}", [P, 2, D]) for u in range(2)]
        ps_log = m.ps("ps_log", [P, 512])
        weights, loaded, stored = m.sem("weights"), m.sem("loaded"), m.sem("stored")
        slot_waited = m.sem("slot_waited")
        moments_ready, rstd_ready, xn_ready = m.sem("moments_ready"), m.sem("rstd_ready"), m.sem("xn_ready")
        turned, xnT_ready, log_ready = m.sem("turned"), m.sem("xnT_ready"), m.sem("log_ready")
        gap_ready, exp_ready = m.sem("gap_ready"), m.sem("exp_ready")
        hidden_made, silu_made = m.sem("hidden_made"), m.sem("silu_made")
        y_made, y_taken, x_new = m.sem("y_made"), m.sem("y_taken"), m.sem("x_new")
        src_g, dst_g = (a.rearrange("(g t p) d -> g p t d", t=GT, p=P) for a in (src, dst))
        flag = const["flag"][0:1, stage:stage + 1]
        ctx.callback(m.free_sems)
        block = ctx.enter_context(nc.Block())

        @block.sync
        def _(sp):
            with only_if(sp, flag):
                sp.dma_start(gate[:], io["gate0T"].rearrange("(c p) e -> p c e", p=P)).then_inc(weights, 16)
                sp.dma_start(w1[:], io["w1T"].rearrange("e (c p) f -> p e c f", p=P)).then_inc(weights, 16)
                sp.dma_start(w2[:], io["w2T"].rearrange("e (c p) f -> p e c f", p=P)).then_inc(weights, 16)
                sp.dma_start(b1[:], io["b1"]).then_inc(weights, 16)
                sp.dma_start(b2[:], io["b2"]).then_inc(weights, 16)
                with sp.Fori(0, n_groups) as g:
                    sp.dma_start(x[:], src_g[bass.ds(g, 1)].squeeze(0)).then_inc(loaded, 16)
                    sp.wait_ge(x_new, g + 1)
                    sp.dma_start(dst_g[bass.ds(g, 1)].squeeze(0), x[:]).then_inc(stored, 16)
                    sp.wait_ge(stored, g * 16 + 16)
                    sp.sem_inc(slot_waited, 1)

        @block.tensor
        def _(pe):
            with only_if(pe, flag):
                pe.wait_ge(weights, 80)
                with pe.Fori(0, n_groups) as g:
                    pe.wait_ge(xn_ready, g + 1)
                    for c in range(DC):
                        for t in range(GT):
                            last = pe.transpose(psT[c][:, t * P:(t + 1) * P], xn[:, t, c * P:(c + 1) * P],
                                                const["ident"][:])
                        last.then_inc(turned, 1)
                    pe.wait_ge(xnT_ready, g * DC + DC)
                    for t in range(GT):
                        for c in range(DC):
                            last = pe.matmul(ps_log[:, t * E0:(t + 1) * E0], xnT[:, c, t * P:(t + 1) * P],
                                             gate[:, c, :], start=(c == 0), stop=(c == DC - 1))
                    last.then_inc(log_ready, 1)
                    for e in range(E0):
                        n = g * (E0 * 2) + e * 2
                        for f in range(DC):
                            pe.wait_ge(silu_made, n + f + 1)
                            for c in range(DC):
                                last = pe.matmul(psH[f][:], w1[:, e, c, f * P:(f + 1) * P], xnT[:, c, :],
                                                 start=(c == 0), stop=(c == DC - 1))
                            last.then_inc(hidden_made, 1)
                        pe.wait_ge(silu_made, n + 4)
                        for u in range(2):
                            pe.wait_ge(y_taken, n + u + 1)
                            for t in range(2):
                                tok = slice((2 * u + t) * P, (2 * u + t + 1) * P)
                                for f in range(DC):
                                    last = pe.matmul(psY[u][:, t, :], hidden[:, f, tok], w2[:, e, f, :],
                                                     start=(f == 0), stop=(f == DC - 1))
                            last.then_inc(y_made, 1)

        @block.scalar
        def _(act):
            with only_if(act, flag):
                act.sem_inc(silu_made, 2)
                act.wait_ge(weights, 80)
                with act.Fori(0, n_groups) as g:
                    for c in range(DC):
                        act.wait_ge(turned, g * DC + c + 1)
                        act.activation(xnT[:, c, :], psT[c][:], ACT.Copy).then_inc(xnT_ready, 1)
                    act.wait_ge(gap_ready, g + 1)
                    act.activation(share[:], share[:], ACT.Exp).then_inc(exp_ready, 1)
                    for e in range(E0):
                        n = g * (E0 * 2) + e * 2
                        act.wait_ge(y_taken, n + 2)
                        for f in range(DC):
                            act.wait_ge(hidden_made, n + f + 1)
                            act.activation(hidden[:, f, :], psH[f][:], ACT.Silu, bias=b1[:, e, f:f + 1])\
                               .then_inc(silu_made, 1)

        @block.gpsimd
        def _(pool):
            with only_if(pool, flag):
                with pool.Fori(0, n_groups) as g:
                    pool.wait_ge(moments_ready, g + 1)
                    norm_rstd(pool, moments, var_eps[:], rstd[:], const["eps"][:],
                              const["minus_half"][:]).then_inc(rstd_ready, 1)

        @block.vector
        def _(dve):
            with only_if(dve, flag):
                dve.sem_inc(y_taken, 2)
                dve.wait_ge(weights, 80)
                with dve.Fori(0, n_groups) as g:
                    rows = lambda t: x[:, t, :]
                    dve.wait_ge(loaded, g * 16 + 16)
                    norm_stats(dve, rows, stats, moments).then_inc(moments_ready, 1)
                    dve.wait_ge(rstd_ready, g + 1)
                    norm_apply(dve, xn, rows, moments, rstd).then_inc(xn_ready, 1)
                    dve.wait_ge(log_ready, g + 1)
                    dve.tensor_copy(logits[:], ps_log[:, 0:GT * E0])
                    dve.drain()
                    for t in range(GT):
                        dve.max(best[:, t, :], logits[:, t, :])
                    dve.drain()
                    for t in range(GT):
                        dve.max_index(best_at[:, t, :], best[:, t, :], logits[:, t, :])
                    dve.tensor_tensor(share[:], logits[:], best[:, :, 0:1].to_broadcast([P, GT, E0]), ALU.subtract)\
                       .then_inc(gap_ready, 1)
                    dve.drain()
                    for k, chosen in ((0, chosen0), (1, chosen1)):
                        dve.tensor_tensor(chosen[:], const["iota0"][:],
                                          best_at[:, :, k:k + 1].to_broadcast([P, GT, E0]), ALU.is_equal)
                    dve.drain()
                    dve.tensor_tensor(chosen0[:], chosen0[:], chosen1[:], ALU.add)
                    dve.drain()
                    dve.tensor_tensor(chosen0[:], chosen0[:],
                                      row_bcast(const["keep"][:, stage, :], GT, [P, GT, E0]), ALU.mult)
                    dve.wait_ge(exp_ready, g + 1)
                    dve.tensor_reduce(total[:], share[:], AX.X, ALU.add)
                    dve.drain()
                    dve.tensor_tensor(share[:], share[:], chosen0[:], ALU.mult)
                    dve.reciprocal(inv_total[:], total[:])
                    dve.drain()
                    dve.tensor_scalar(inv_total[:], inv_total[:], 0.5, None, ALU.mult)
                    dve.drain()
                    dve.tensor_tensor(share[:], share[:], inv_total[:].unsqueeze(2).to_broadcast([P, GT, E0]),
                                      ALU.mult)
                    for e in range(E0):
                        for u in range(2):
                            dve.wait_ge(y_made, g * (E0 * 2) + e * 2 + u + 1)
                            dve.tensor_tensor(y[:], psY[u][:], row_bcast(b2[:, e, :], 2, [P, 2, D]), ALU.add)\
                               .then_inc(y_taken, 1)
                            dve.drain()
                            for t in range(2):
                                dve.tensor_scalar(y[:, t, :], y[:, t, :], share[:, 2 * u + t, e:e + 1], None, ALU.mult)
                            dve.drain()
                            last = dve.tensor_tensor(x[:, 2 * u:2 * u + 2, :], x[:, 2 * u:2 * u + 2, :], y[:], ALU.add)
                            if e == E0 - 1 and u == 1:
                                last.then_inc(x_new, 1)
                            else:
                                dve.drain()


TAIL = STEPS
PREP = {
    2: [("stats", 0)], 3: [("stats", 1), ("norm", 0)], 4: [("turn", 0)], 5: [("turn", 1)], 6: [("norm", 1)],
    7: [("turn", 2), ("bias", 0)], 8: [("turn", 3)], 9: [("zg", 0)], 10: [("zg", 1)], 11: [("zg", 2)],
    12: [("zg", 3)], 13: [("route", 0)], 15: [("weigh", 0)], 17: [("zturn", 0)], 18: [("zturn", 1)],
    19: [("y", 0)], 20: [("y", 1)], 21: [("y", 2), ("stats", 2)], 22: [("y", 3), ("norm", 2)],
    23: [("turn", 4), ("stats", 3)], 24: [("turn", 5)], 25: [("norm", 3)], 26: [("turn", 6)], 27: [("turn", 7)],
    28: [("qk", 0)], 29: [("qk", 1), ("high", 0)], 30: [("mid", 0)], 31: [("qk", 2), ("low", 0)],
    32: [("qk", 3), ("high", 1)], 33: [("mid", 1)], 34: [("qk", 4), ("low", 1)],
    35: [("qk", 5), ("high", 2)], 36: [("mid", 2)], 37: [("qk", 6), ("low", 2)],
    38: [("qk", 7), ("high", 3)], 39: [("mid", 3)], 40: [("low", 3)],
    TAIL: [("v", 0), ("v", 1), ("v", 2), ("v", 3)],
}
POST = {
    0: [("wo", 0)], 1: [("wo", 1)], 2: [("wo", 2), ("stats", 0)], 3: [("wo", 3)], 4: [("stats", 1), ("norm", 0)],
    6: [("turn", 0)], 7: [("turn", 1)], 8: [("norm", 1)], 9: [("turn", 2), ("bias", 0)], 10: [("turn", 3)],
    11: [("zg", 0)], 12: [("zg", 1)], 13: [("zg", 2)], 14: [("zg", 3)], 15: [("route", 0)], 17: [("weigh", 0)],
    19: [("zturn", 0)], 20: [("zturn", 1)], 21: [("y", 0)], 22: [("y", 1)], 23: [("y", 2)], 24: [("y", 3)],
    25: [("store", 0)],
}
BANKED = {"turn", "zg", "zturn", "y", "qk", "v", "wo", "denom"}
SLOT_OF, SLOT_END = [], []
for _hg in range(NHG):
    for _qc in range(NQC):
        SLOT_OF += [(_hg, _qc, _kb) for _kb in range(KQ * (_qc + 1))]
        SLOT_END.append(len(SLOT_OF) - 1)
NSLOTS = len(SLOT_END)
HGSTEPS = STEPS // NHG
COPY_AT = {min(e + 1, TAIL): n for n, e in enumerate(SLOT_END)}
DENOM_AT = {min(e + 2, TAIL): n for n, e in enumerate(SLOT_END)}


def banked(table):
    return sum(kind in BANKED for items in table.values() for kind, _ in items)


N_PREP, N_POST = banked(PREP), banked(POST)


class Uses:

    def __init__(self):
        self.base, self.k = 0, 0

    def next(self):
        self.k += 1
        return self.base + self.k

    def so_far(self):
        return self.base + self.k

    def enter(self, turns, per_turn):
        self.start = self.base + self.k
        self.base, self.k = turns * per_turn + self.start, 0

    def leave(self, turns, per_turn):
        self.base, self.k = self.start + turns * per_turn, 0


def row_max_pass(nc, io, const):
    NB = io["tokens"] // S
    with ExitStack() as ctx:
        m = Pools(nc, ctx, "m_")
        q_rows, k_rows = m.sb("q_rows", [ROWS, HG, S], BF16), m.sb("k_rows", [ROWS, HG, S], BF16)
        identb, mask = m.sb("identb", [P, P], BF16), m.sb("mask", [P, P], BF16)
        row_max, row_maxT = m.sb("row_max", [P, HG * TS]), m.sb("row_maxT", [HG * TS, P])
        rest, part = m.sb("rest", [HG * TS, P]), m.sb("part", [HG * TS, 3, P], BF16)
        s_tile = [m.ps(f"s_tile{k}", [P, S]) for k in range(2)]
        turned = m.ps("turned", [P, QC])
        rows_loaded, part_stored, tabled = m.sem("rows_loaded"), m.sem("part_stored"), m.sem("tabled")
        scored, maxed, max_ready = m.sem("scored"), m.sem("maxed"), m.sem("max_ready")
        max_turned, part_ready, waited = m.sem("max_turned"), m.sem("part_ready"), m.sem("waited")
        parts_r = io["parts"].rearrange("b a c e (i g j) t -> b g a (c e i) (j t)", g=NHG, j=HG)
        shift_w = io["shift"].rearrange("b c (g j) (u p) -> b g (j u) c p", j=HG, p=P)
        flag = const["flag"][0:1, 2:3]
        NSC = HG * TS
        ctx.callback(m.free_sems)
        block = ctx.enter_context(nc.Block())

        @block.sync
        def _(sp):
            with only_if(sp, flag):
                with sp.Fori(0, NB) as b:
                    for hg in range(NHG):
                        src = parts_r[bass.ds(b, 1)].squeeze(0)[hg]
                        for a, buf in ((0, q_rows), (1, k_rows)):
                            for slot, c, n in RUNS[a]:
                                sp.dma_start(buf[slot * HD:(slot + n) * HD].rearrange("r h t -> r (h t)"),
                                             src[a, c * HD:(c + n) * HD]).then_inc(rows_loaded, 16)
                        sp.wait_ge(part_ready, b * NHG + hg + 1)
                        for c in range(3):
                            sp.dma_start(shift_w[bass.ds(b, 1)].squeeze(0)[hg, :, c], part[:, c, :])\
                              .then_inc(part_stored, 16)
                        sp.wait_ge(part_stored, (b * NHG + hg) * 48 + 48)
                        sp.sem_inc(waited, 1)

        @block.gpsimd
        def _(pool):
            with only_if(pool, flag):
                pool.memset(identb[:], 0.0)
                pool.memset(mask[:], 0.0)
                pool.drain()
                pool.affine_select(out=identb[:], in_=identb[:], compare_op=ALU.not_equal, fill=1.0,
                                   base=0, pattern=[[-1, P]], channel_multiplier=1)
                pool.affine_select(out=mask[:], in_=mask[:], compare_op=ALU.is_ge, fill=MASKED,
                                   base=0, pattern=[[-1, P]], channel_multiplier=1)
                pool.drain()
                pool.sem_inc(tabled, 1)

        @block.tensor
        def _(pe):
            with only_if(pe, flag):
                pe.wait_ge(tabled, 1)
                with pe.Fori(0, NB) as b:
                    for hg in range(NHG):
                        base = (b * NHG + hg) * NSC
                        pe.wait_ge(rows_loaded, (b * NHG + hg) * 112 + 112)
                        for n in range(NSC):
                            h, qt = n // TS, n % TS
                            tile = s_tile[n % 2]
                            if n >= 2:
                                pe.wait_ge(maxed, base + n - 1)
                            for k0 in range(0, (qt + 1) * P, QC):
                                k1 = min(k0 + QC, (qt + 1) * P)
                                pe.matmul(tile[:, k0:k1], q_rows[:, h, qt * P:(qt + 1) * P], k_rows[:, h, k0:k1],
                                          start=True, stop=True)
                            pe.matmul(tile[:, qt * P:(qt + 1) * P], identb[:], mask[:], start=False, stop=True,
                                      skip_group_check=True).then_inc(scored, 1)
                        pe.wait_ge(max_ready, b * NHG + hg + 1)
                        pe.transpose(turned[0:NSC, 0:P], row_max[:], const["ident"][:]).then_inc(max_turned, 1)

        @block.vector
        def _(dve):
            with only_if(dve, flag):
                with dve.Fori(0, NB) as b:
                    for hg in range(NHG):
                        base = (b * NHG + hg) * NSC
                        for n in range(NSC):
                            qt = n % TS
                            dve.wait_ge(scored, base + n + 1)
                            dve.tensor_reduce(row_max[:, n:n + 1], s_tile[n % 2][:, 0:(qt + 1) * P], AX.X, ALU.max)\
                               .then_inc(maxed, 1)
                        dve.drain()
                        dve.sem_inc(max_ready, 1)
                        dve.wait_ge(max_turned, b * NHG + hg + 1)
                        dve.tensor_scalar(row_maxT[:], turned[0:NSC, 0:P], -1.0, None, ALU.mult)
                        dve.drain()
                        dve.tensor_copy(part[:, 0, :], row_maxT[:])
                        dve.drain()
                        dve.tensor_tensor(rest[:], row_maxT[:], part[:, 0, :], ALU.subtract)
                        dve.drain()
                        dve.tensor_copy(part[:, 1, :], rest[:])
                        dve.drain()
                        dve.tensor_tensor(part[:, 2, :], rest[:], part[:, 1, :], ALU.subtract).then_inc(part_ready, 1)


def sequence_pass(nc, io, const, shifted):
    NB = io["tokens"] // S
    n_rows = ROWS + (3 if shifted else 0)
    per_rows = 16 * (8 if shifted else 7)
    flag = const["flag"][0:1, 2:3] if shifted else None
    with ExitStack() as ctx:
        m = Pools(nc, ctx, "r_" if shifted else "s_")
        x = m.sb("x", [P, 3, TS, D])
        w_ag, w_base, w_b = m.sb("w_ag", [P, DC, NZG]), m.sb("w_base", [P, DC, D]), m.sb("w_b", [P, D])
        half_b = m.sb("half_b", [P, D])
        w_qk = m.sb("w_qk", [P, 2, DC, D])
        w_v, w_o = m.sb("w_v", [P, DC, D]), m.sb("w_o", [P, NHG, D])
        cos, sin = m.sb("cos", [P, S]), m.sb("sin", [P, S])
        identb, mask = m.sb("identb", [P, P], BF16), m.sb("mask", [P, P], BF16)
        spread = m.sb("spread", [P, P])
        q_rows, k_rows = m.sb("q_rows", [n_rows, 2, HG, S], BF16), m.sb("k_rows", [n_rows, 2, HG, S], BF16)
        v = m.sb("v", [P, TS * H * VW + 16])
        v_heads = v[:, 0:TS * H * VW].rearrange("p (t h w) -> p t h w", t=TS, w=VW)
        probs = m.sb("probs", [P, 2, HG, QC])
        sums, recip = m.sb("sums", [P, 2, QC]), m.sb("recip", [P, QC])
        attn = m.sb("attn", [P, NHG, S])
        rope = m.sb("rope", [P, 4, QC])
        turned_qk, rest = m.sb("turned_qk", [P, 2, QC]), m.sb("rest", [P, 2, QC])
        part = [m.sb(f"part{c}", [P, 2, QC], BF16) for c in range(3)]
        seen = m.sb("seen", [P, 2, QC])
        iota = m.sb("iota", [P, NT])

        s_tile = [m.ps(f"s_tile{p}", [P, 2, QC]) for p in range(2)]
        o_bank = [m.ps(f"o_bank{p}", [P, QC]) for p in range(2)]

        class Side:

            def __init__(self, name, norms):
                self.norms = norms
                self.xn, self.xnT = m.sb(name + "xn", [P, GT, D]), m.sb(name + "xnT", [P, DC, S])
                self.stats = [m.sb(f"{name}stats{g}", [P, GT, 6]) for g in range(2)]
                self.moments = [m.sb(f"{name}moments{g}", [P, GT, 2]) for g in range(2)]
                self.var_eps, self.rstd = m.sb(name + "var_eps", [P, 2, GT]), m.sb(name + "rstd", [P, 2, GT])
                self.zg, self.zT = m.sb(name + "zg", [P, TS, NZG]), m.sb(name + "zT", [P, S])
                self.best, self.best_at = m.sb(name + "best", [P, TS, 8]), m.sb(name + "best_at", [P, TS, 8], U32)
                self.c0, self.c1 = m.sb(name + "c0", [P, TS, NT]), m.sb(name + "c1", [P, TS, NT])
                self.gap, self.den = m.sb(name + "gap", [P, TS, NT]), m.sb(name + "den", [P, 3, TS])
                self.bank = m.ps(name + "bank", [P, QC])
                self.full, self.free = m.sem(name + "full"), m.sem(name + "free")
                self.moments_ready, self.rstd_ready = m.sem(name + "moments_ready"), m.sem(name + "rstd_ready")
                self.xn_ready = m.sem(name + "xn_ready")
                self.biased, self.gap_ready = m.sem(name + "biased"), m.sem(name + "gap_ready")
                self.exp_ready, self.z_ready = m.sem(name + "exp_ready"), m.sem(name + "z_ready")

        prep, post = Side("prep_", 4), Side("post_", 2)
        weights, tabled, halved = m.sem("weights"), m.sem("tabled"), m.sem("halved")
        x_loaded, x_stored = m.sem("x_loaded"), m.sem("x_stored")
        scored = [m.sem(f"scored{p}") for p in range(2)]
        exped = [m.sem(f"exped{p}") for p in range(2)]
        used, copied = m.sem("used"), m.sem("copied")
        checked, rotated, attn_ready = m.sem("checked"), m.sem("rotated"), m.sem("attn_ready")
        part_ready = [m.sem(f"part_ready{c}") for c in range(3)]
        part_stored = [m.sem(f"part_stored{c}") for c in range(3)]
        rest_ready = m.sem("rest_ready")
        rows_loaded = [m.sem(f"rows_loaded{k}") for k in range(2)]
        in_range, out_of_range = m.sb("in_range", [P, 2]), m.sb("out_of_range", [P, 3])
        seen_ready, spread_seen, ones_ready = m.sem("seen_ready"), m.sem("spread_seen"), m.sem("ones_ready")
        in_range_ready, range_summed = m.sem("in_range_ready"), m.sem("range_summed")

        x_in = io["x_mix"].rearrange("(b t p) d -> b p t d", t=TS, p=P)
        x_out = io["out"].rearrange("(b t p) d -> b p t d", t=TS, p=P)
        parts_w = io["parts"].rearrange("b a c e r t -> b a c r e t")
        parts_r = io["parts"].rearrange("b a c e (i h) t -> b a (c e i) (h t)", h=H)

        def dram_at(vw, b):
            return vw[b] if isinstance(b, int) else vw[bass.ds(b, 1)].squeeze(0)

        def sequences(eng, iteration, uses_a, uses_b):
            iteration(None, 0, None)
            iteration(0, 1, None)
            with eng.Fori(1, NB - 1) as b:
                uses_a.enter(b - 1, N_PREP)
                uses_b.enter(b - 1, N_POST + NSLOTS)
                iteration(b, b + 1, b - 1)
            uses_a.leave(NB - 2, N_PREP)
            uses_b.leave(NB - 2, N_POST + NSLOTS)
            iteration(NB - 1, None, NB - 2)
            iteration(None, None, NB - 1)

        ctx.callback(m.free_sems)
        block = ctx.enter_context(nc.Block())

        @block.sync
        def _(sp):
            with only_if(sp, flag):
                bank_b = Uses()
                sp.sem_inc(x_stored, 16)
                for buf, name in ((w_ag, "w_agT"), (w_base, "w_baseT"), (w_v, "w_vT")):
                    sp.dma_start(buf[:], io[name].rearrange("(c p) e -> p c e", p=P)).then_inc(weights, 16)
                sp.dma_start(w_qk[:, 0], io["w_qT"].rearrange("(c p) e -> p c e", p=P)).then_inc(weights, 16)
                sp.dma_start(w_qk[:, 1], io["w_kT"].rearrange("(c p) e -> p c e", p=P)).then_inc(weights, 16)
                for buf, name in ((w_b, "w_b"), (half_b, "base_b"), (cos, "cos"), (sin, "sin")):
                    sp.dma_start(buf[:], io[name]).then_inc(weights, 16)
                sp.wait_ge(tabled, 1)
                for hg in range(NHG):
                    for j in range(HG):
                        h = hg * HG + j
                        sp.dma_start(w_o[32 * j:32 * j + HD, hg, :],
                                     io["w_oT"][h * HD:(h + 1) * HD, :]).then_inc(weights, 16)

                def rows(b, hg):
                    k = hg % 2
                    if not (isinstance(b, int) and b == 0 and hg < 2):
                        sp.wait_ge(used, b * STEPS + HGSTEPS * (hg - 1) + 2)
                    span = slice(hg * HG * S, (hg + 1) * HG * S)
                    for a, buf in ((0, q_rows), (1, k_rows)):
                        for slot, c, n in RUNS[a]:
                            sp.dma_start(buf[slot * HD:(slot + n) * HD, k, :, :].rearrange("r h t -> r (h t)"),
                                         dram_at(parts_r, b)[a, c * HD:(c + n) * HD, span]).then_inc(rows_loaded[k], 16)
                    if shifted:
                        sp.dma_start(q_rows[ROWS:n_rows, k], dram_at(io["shift"], b)[:, hg * HG:(hg + 1) * HG, :])\
                          .then_inc(rows_loaded[k], 16)

                def store_part(b, j, c):
                    a, g = j % 2, j // 2
                    sp.wait_ge(part_ready[c], b * 4 + j + 1)
                    sp.dma_start(dram_at(parts_w, b)[a, c, :, :, g * QC:(g + 1) * QC], part[c][:]).then_inc(part_stored[c], 16)

                def iteration(b, p, q):
                    for s in range(STEPS + 1):
                        if s == 0 and p is not None:
                            if not isinstance(p, int) or p >= 3:
                                sp.wait_ge(x_stored, (p - 1) * 16)
                            sp.dma_start(at(x, p % 3), dram_at(x_in, p)).then_inc(x_loaded, 16)
                        if b is not None and s in (HGSTEPS, 2 * HGSTEPS):
                            rows(b, s // HGSTEPS + 1)
                        if p is not None:
                            for kind, j in PREP.get(s, ()):
                                if kind == "high":
                                    store_part(p, j, 0)
                                if kind == "mid":
                                    store_part(p, j, 1)
                                if kind == "low":
                                    store_part(p, j, 2)
                                    if j == 3:
                                        for c in range(3):
                                            sp.wait_ge(part_stored[c], p * 64 + 64)
                                        rows(p, 0)
                        if q is not None:
                            for kind, _ in POST.get(s, ()):
                                if kind in BANKED:
                                    bank_b.next()
                                if kind == "store":
                                    sp.wait_ge(post.free, bank_b.so_far() + 1)
                                    sp.dma_start(dram_at(x_out, q), at(x, q % 3)).then_inc(x_stored, 16)
                        if b is not None and s in DENOM_AT:
                            bank_b.next()
                    if p is not None:
                        rows(p, 1)

                sequences(sp, iteration, Uses(), bank_b)
                sp.wait_ge(x_stored, 16 * NB + 16)

        @block.tensor
        def _(pe):
            with only_if(pe, flag):
                bank_a, bank_b = Uses(), Uses()

                def fill(side, uses):
                    n = uses.next()
                    pe.wait_ge(side.free, n)

                def side_item(side, uses, kind, k, b):
                    if kind in BANKED:
                        fill(side, uses)
                    if kind == "turn":
                        g, c = k // 2, k % 2
                        pe.wait_ge(side.xn_ready, b * side.norms + g + 1)
                        for t in range(GT):
                            last = pe.transpose(side.bank[:, t * P:(t + 1) * P], side.xn[:, t, c * P:(c + 1) * P],
                                                const["ident"][:])
                        last.then_inc(side.full, 1)
                    if kind == "zg":
                        for t in range(2):
                            for c in range(DC):
                                last = pe.matmul(side.bank[:, t * NZG:(t + 1) * NZG],
                                                 side.xnT[:, c, (2 * k + t) * P:(2 * k + t + 1) * P], w_ag[:, c, :],
                                                 start=(c == 0), stop=(c == DC - 1))
                        last.then_inc(side.full, 1)
                    if kind == "zturn":
                        pe.wait_ge(side.z_ready, b + 1)
                        for t in range(GT):
                            last = pe.transpose(side.bank[:, t * P:(t + 1) * P], side.zg[:, GT * k + t, 0:NZ],
                                                const["ident"][:])
                        last.then_inc(side.full, 1)
                    if kind == "y":
                        for t in range(2):
                            tok = slice((2 * k + t) * P, (2 * k + t + 1) * P)
                            for c in range(DC):
                                pe.matmul(side.bank[:, t * D:(t + 1) * D], side.xnT[:, c, tok], w_base[:, c, :],
                                          start=(c == 0), stop=False)
                            last = pe.matmul(side.bank[:, t * D:(t + 1) * D], side.zT[:, tok], w_b[:],
                                             start=False, stop=True)
                        last.then_inc(side.full, 1)
                    if kind == "qk":
                        j, eo = k // 2, k % 2
                        a, g = j % 2, j // 2
                        for c in range(DC):
                            last = pe.matmul(side.bank[:], w_qk[:, a, c, eo * P:(eo + 1) * P],
                                             side.xnT[:, c, g * QC:(g + 1) * QC], start=(c == 0), stop=(c == DC - 1))
                        last.then_inc(side.full, 1)
                    if kind == "v":
                        for t in range(2):
                            for c in range(DC):
                                last = pe.matmul(side.bank[:, t * D:(t + 1) * D],
                                                 side.xnT[:, c, (2 * k + t) * P:(2 * k + t + 1) * P], w_v[:, c, :],
                                                 start=(c == 0), stop=(c == DC - 1))
                        last.then_inc(side.full, 1)
                    if kind == "wo":
                        pe.wait_ge(attn_ready, b * NSLOTS + NSLOTS)
                        for t in range(2):
                            for hg in range(NHG):
                                last = pe.matmul(side.bank[:, t * D:(t + 1) * D],
                                                 attn[:, hg, (2 * k + t) * P:(2 * k + t + 1) * P], w_o[:, hg, :],
                                                 start=(hg == 0), stop=(hg == NHG - 1))
                        last.then_inc(side.full, 1)

                def score(b, s):
                    hg, qc, kb = SLOT_OF[s]
                    off = max(kb - KQ * qc, 0) * P
                    if s % HGSTEPS == 0:
                        pe.wait_ge(rows_loaded[hg % 2], (b * 2 + hg // 2 + 1) * per_rows)
                    for p in range(2):
                        pe.wait_ge(exped[p], b * STEPS + s + 1)
                        for j in range(2):
                            h = 2 * p + j
                            last = pe.matmul(s_tile[p][:, j, off:QC], k_rows[:, hg % 2, h, kb * P:(kb + 1) * P],
                                             q_rows[:, hg % 2, h, qc * QC + off:(qc + 1) * QC],
                                             start=True, stop=True)
                            if kb >= KQ * qc:
                                last = pe.matmul(s_tile[p][:, j, off:off + P], mask[:], identb[:],
                                                 start=False, stop=True, skip_group_check=True)
                        last.then_inc(scored[p], 1)

                def weigh_v(b, s):
                    hg, qc, kb = SLOT_OF[s]
                    n = hg * NQC + qc
                    off = max(kb - KQ * qc, 0) * P
                    if s == 0:
                        pe.wait_ge(prep.free, bank_a.so_far() + 1)
                    if kb == 0:
                        pe.wait_ge(copied, b * NSLOTS + n + 1)
                    for p in range(2):
                        pe.wait_ge(exped[p], b * STEPS + s + 2)
                    for h in range(HG):
                        col = (kb * H + hg * HG + h) * VW
                        last = pe.matmul(o_bank[n % 2][32 * h:32 * h + 32, off:QC], v[:, col:col + 32],
                                         probs[:, s % 2, h, off:QC], start=(kb == 0), stop=(kb >= KQ * qc),
                                         skip_group_check=True)
                    last.then_inc(used, 1)

                def iteration(b, p, q):
                    if b is not None:
                        score(b, 0)
                    for s in range(STEPS + 1):
                        if b is not None and s + 1 < STEPS:
                            score(b, s + 1)
                        if p is not None:
                            for kind, k in PREP.get(s, ()):
                                side_item(prep, bank_a, kind, k, p)
                        if q is not None:
                            for kind, k in POST.get(s, ()):
                                side_item(post, bank_b, kind, k, q)
                        if b is not None and s in DENOM_AT:
                            n = DENOM_AT[s]
                            fill(post, bank_b)
                            pe.wait_ge(copied, b * NSLOTS + n + 3)
                            pe.matmul(post.bank[:], spread[:], sums[:, n % 2, :], start=True, stop=True)\
                              .then_inc(post.full, 1)
                        if b is not None and s < STEPS:
                            weigh_v(b, s)

                pe.wait_ge(weights, 16 * (9 + H))
                pe.wait_ge(halved, 1)
                pe.wait_ge(tabled, 2)
                if shifted:
                    pe.wait_ge(ones_ready, 1)
                pe.sem_inc(used, 2)
                sequences(pe, iteration, bank_a, bank_b)
                if not shifted:
                    pe.wait_ge(copied, NB * NSLOTS + 2)
                    pe.wait_ge(seen_ready, 1)
                    for c in range(2):
                        pe.matmul(o_bank[c][:], spread[:], seen[:, c, :], start=True, stop=True)\
                          .then_inc(spread_seen, 1)
                    pe.wait_ge(in_range_ready, 1)
                    pe.matmul(prep.bank[:, 0:2], const["ones"][:], in_range[:], start=True, stop=True)\
                      .then_inc(range_summed, 1)

        @block.scalar
        def _(act):
            with only_if(act, flag):
                bank_a, bank_b = Uses(), Uses()

                def side_item(side, uses, kind, k, b):
                    n = uses.next() if kind in BANKED else None
                    if kind == "turn":
                        act.wait_ge(side.full, n)
                        g, c = (k // 2) % 2, k % 2
                        act.activation(side.xnT[:, c, g * QC:(g + 1) * QC], side.bank[:], ACT.Copy)\
                           .then_inc(side.free, 1)
                    if kind == "zturn":
                        act.wait_ge(side.full, n)
                        act.activation(side.zT[:, k * QC:(k + 1) * QC], side.bank[:], ACT.Copy)\
                           .then_inc(side.free, 1)
                    if kind == "route":
                        act.wait_ge(side.gap_ready, b + 1)
                        act.activation(side.gap[:], side.gap[:], ACT.Exp).then_inc(side.exp_ready, 1)
                    if kind == "high":
                        act.wait_ge(rotated, b * 4 + k + 1)
                        if not isinstance(b, int) or b * 4 + k > 0:
                            act.wait_ge(part_stored[0], (b * 4 + k) * 16)
                        act.activation(part[0][:], turned_qk[:], ACT.Copy).then_inc(part_ready[0], 1)
                    if kind == "mid":
                        act.wait_ge(rest_ready, b * 4 + k + 1)
                        if not isinstance(b, int) or b * 4 + k > 0:
                            act.wait_ge(part_stored[1], (b * 4 + k) * 16)
                        act.activation(part[1][:], rest[:], ACT.Copy).then_inc(part_ready[1], 1)

                def exps(b, s):
                    hg, qc, kb = SLOT_OF[s]
                    off = max(kb - KQ * qc, 0) * P
                    act.wait_ge(used, b * STEPS + s + 1)
                    for p in range(2):
                        act.wait_ge(scored[p], b * STEPS + s + 1)
                        act.activation(probs[:, s % 2, 2 * p:2 * p + 2, off:QC], s_tile[p][:, :, off:QC], ACT.Exp,
                                       scale=float(HD) ** -0.5).then_inc(exped[p], 1)

                def items(b, p, q, s):
                    if p is not None:
                        for kind, k in PREP.get(s, ()):
                            side_item(prep, bank_a, kind, k, p)
                    if q is not None:
                        for kind, k in POST.get(s, ()):
                            side_item(post, bank_b, kind, k, q)
                    if b is not None and s in DENOM_AT:
                        bank_b.next()

                def iteration(b, p, q):
                    for s in range(STEPS + 1):
                        if b is not None and s < STEPS:
                            exps(b, s)
                        if s > 0:
                            items(b, p, q, s - 1)
                    items(b, p, q, STEPS)

                for p in range(2):
                    act.sem_inc(exped[p], 1)
                sequences(act, iteration, bank_a, bank_b)

        @block.gpsimd
        def _(pool):
            with only_if(pool, flag):
                bank_a, bank_b = Uses(), Uses()

                def side_item(side, uses, kind, k, b):
                    if kind in BANKED:
                        uses.next()
                    if kind == "stats":
                        pool.wait_ge(side.moments_ready, b * side.norms + k + 1)
                        norm_rstd(pool, side.moments[k % 2], side.var_eps[:, k % 2], side.rstd[:, k % 2],
                                  const["eps"][:], const["minus_half"][:]).then_inc(side.rstd_ready, 1)
                    if kind == "bias":
                        pool.wait_ge(side.xn_ready, b * side.norms + 2)
                        pool.tensor_tensor(at(x, b % 3), at(x, b % 3), row_bcast(half_b[:], TS, [P, TS, D]),
                                           ALU.add).then_inc(side.biased, 1)
                    if kind == "high":
                        pool.wait_ge(side.free, uses.so_far() + 1)
                        if not isinstance(b, int) or b * 4 + k > 0:
                            pool.wait_ge(part_ready[0], b * 4 + k)
                        pool.tensor_tensor(turned_qk[:, 0, :], rope[:, 0, :], rope[:, 2, :], ALU.subtract)
                        pool.tensor_tensor(turned_qk[:, 1, :], rope[:, 1, :], rope[:, 3, :], ALU.add).then_inc(rotated, 1)
                    if kind == "mid":
                        pool.wait_ge(part_ready[0], b * 4 + k + 1)
                        if not isinstance(b, int) or b * 4 + k > 0:
                            pool.wait_ge(part_ready[1], b * 4 + k)
                        pool.tensor_tensor(rest[:], turned_qk[:], part[0][:], ALU.subtract).then_inc(rest_ready, 1)
                    if kind == "low":
                        pool.wait_ge(part_ready[1], b * 4 + k + 1)
                        if not isinstance(b, int) or b * 4 + k > 0:
                            pool.wait_ge(part_stored[2], (b * 4 + k) * 16)
                        pool.tensor_tensor(part[2][:], rest[:], part[1][:], ALU.subtract).then_inc(part_ready[2], 1)

                def iteration(b, p, q):
                    for s in range(STEPS + 1):
                        if p is not None:
                            for kind, k in PREP.get(s, ()):
                                side_item(prep, bank_a, kind, k, p)
                        if q is not None:
                            for kind, k in POST.get(s, ()):
                                side_item(post, bank_b, kind, k, q)
                        if b is not None and s in DENOM_AT:
                            n = DENOM_AT[s]
                            pool.wait_ge(post.free, bank_b.next() + 1)
                            pool.tensor_tensor(seen[:, 0, :], seen[:, 0, :], sums[:, n % 2, :], ALU.add)
                            pool.tensor_tensor(seen[:, 1, :], seen[:, 1, :], recip[:], ALU.add).then_inc(checked, 1)

                pool.memset(w_o[:], 0.0).then_inc(tabled, 1)
                pool.memset(identb[:], 0.0)
                pool.memset(mask[:], 0.0)
                pool.memset(spread[:], 0.0)
                pool.memset(seen[:], 0.0)
                pool.memset(v[:], 1.0)
                pool.iota(iota[:], pattern=[[1, NT]], base=0, channel_multiplier=0, allow_small_or_imprecise_dtypes=True)
                pool.drain()
                pool.affine_select(out=identb[:], in_=identb[:], compare_op=ALU.not_equal, fill=1.0,
                                   base=0, pattern=[[-1, P]], channel_multiplier=1)
                pool.affine_select(out=mask[:], in_=mask[:], compare_op=ALU.is_ge, fill=MASKED,
                                   base=0, pattern=[[-1, P]], channel_multiplier=1)
                for j in range(HG):
                    part_of = spread[:, 32 * j:32 * j + 32]
                    pool.affine_select(out=part_of, in_=part_of, compare_op=ALU.not_equal, fill=1.0,
                                       base=-(32 * j + HD), pattern=[[0, 32]], channel_multiplier=1)
                pool.drain()
                pool.sem_inc(tabled, 1)
                sequences(pool, iteration, bank_a, bank_b)
                pool.drain()
                pool.sem_inc(seen_ready, 1)

        @block.vector
        def _(dve):
            with only_if(dve, flag):
                bank_a, bank_b = Uses(), Uses()

                def side_item(side, uses, kind, k, b):
                    n = uses.next() if kind in BANKED else None
                    xb = at(x, b % 3)
                    if kind == "stats":
                        dve.drain()
                        if side is prep and k == 0:
                            dve.wait_ge(x_loaded, b * 16 + 16)
                        g = k % 2
                        rows = lambda t: at(x, b % 3)[:, GT * g + t, :]
                        norm_stats(dve, rows, side.stats[g], side.moments[g]).then_inc(side.moments_ready, 1)
                    if kind == "norm":
                        g = k % 2
                        dve.wait_ge(side.rstd_ready, b * side.norms + k + 1)
                        before = uses.so_far()
                        if not isinstance(before, int) or before > 0:
                            dve.wait_ge(side.full, before)
                        rows = lambda t: at(x, b % 3)[:, GT * g + t, :]
                        norm_apply(dve, side.xn, rows, side.moments[g], side.rstd[:, g]).then_inc(side.xn_ready, 1)
                    if kind == "zg":
                        dve.wait_ge(side.full, n)
                        dve.tensor_copy(side.zg[:, 2 * k:2 * k + 2, :],
                                        side.bank[:, 0:2 * NZG].rearrange("p (t z) -> p t z", t=2)).then_inc(side.free, 1)
                    if kind == "route":
                        dve.drain()
                        for t in range(TS):
                            dve.max(side.best[:, t, :], side.zg[:, t, NZ:NZG])
                        dve.drain()
                        for t in range(TS):
                            dve.max_index(side.best_at[:, t, :], side.best[:, t, :], side.zg[:, t, NZ:NZG])
                        dve.tensor_tensor(side.gap[:], side.zg[:, :, NZ:NZ + NT],
                                          side.best[:, :, 0:1].to_broadcast([P, TS, NT]), ALU.subtract)\
                           .then_inc(side.gap_ready, 1)
                        dve.drain()
                        for j, chosen in ((0, side.c0), (1, side.c1)):
                            dve.tensor_tensor(chosen[:], row_bcast(iota[:], TS, [P, TS, NT]),
                                              side.best_at[:, :, j:j + 1].to_broadcast([P, TS, NT]), ALU.is_equal)
                        dve.drain()
                        dve.tensor_tensor(side.c0[:], side.c0[:], side.c1[:], ALU.add)
                    if kind == "weigh":
                        dve.drain()
                        dve.wait_ge(side.exp_ready, b + 1)
                        dve.tensor_tensor(side.c0[:], side.c0[:], side.gap[:], ALU.mult)
                        dve.drain()
                        dve.tensor_reduce(side.den[:, 0, :], side.c0[:], AX.X, ALU.add)
                        dve.drain()
                        dve.tensor_scalar(side.den[:, 1, :], side.den[:, 0, :], 0.0, None, ALU.is_equal)
                        dve.drain()
                        dve.tensor_tensor(side.den[:, 0, :], side.den[:, 0, :], side.den[:, 1, :], ALU.add)
                        dve.drain()
                        dve.reciprocal(side.den[:, 2, :], side.den[:, 0, :])
                        dve.drain()
                        dve.tensor_tensor(side.c0[:], side.c0[:], side.den[:, 2, :].unsqueeze(2)
                                          .to_broadcast([P, TS, NT]), ALU.mult)
                        dve.drain()
                        for t in range(TS):
                            z = side.zg[:, t, 0:NZ].rearrange("p (e r) -> p e r", r=RANK)
                            last = dve.tensor_tensor(z, z, side.c0[:, t, :].unsqueeze(2).to_broadcast([P, NT, RANK]),
                                                     ALU.mult)
                        last.then_inc(side.z_ready, 1)
                    if kind in ("y", "wo"):
                        if kind == "y":
                            dve.wait_ge(side.biased, b + 1)
                        dve.wait_ge(side.full, n)
                        tiles = xb[:, 2 * k:2 * k + 2, :]
                        dve.tensor_tensor(tiles, side.bank[:].rearrange("p (t d) -> p t d", t=2), tiles, ALU.add)\
                           .then_inc(side.free, 1)
                    if kind == "qk":
                        j, eo = k // 2, k % 2
                        g = j // 2
                        dve.wait_ge(side.full, n)
                        if not isinstance(b, int) or b * 4 + j > 0:
                            dve.wait_ge(rotated, b * 4 + j)
                        tok = slice(g * QC, (g + 1) * QC)
                        one, two = (cos, sin) if eo == 0 else (sin, cos)
                        dve.tensor_tensor(rope[:, 2 * eo, :], side.bank[:], one[:, tok], ALU.mult)
                        dve.tensor_tensor(rope[:, 2 * eo + 1, :], side.bank[:], two[:, tok], ALU.mult)\
                           .then_inc(side.free, 1)
                    if kind == "v":
                        dve.wait_ge(side.full, n)
                        for t in range(2):
                            last = dve.tensor_copy(v_heads[:, 2 * k + t, :, 0:HD], side.bank[:, t * D:(t + 1) * D]
                                                   .rearrange("p (h w) -> p h w", w=HD))
                        last.then_inc(side.free, 1)

                def copy_sums(b, n):
                    dve.wait_ge(used, b * STEPS + SLOT_END[n] + 3)
                    if not isinstance(b, int) or b * NSLOTS + n >= 2:
                        dve.wait_ge(checked, b * NSLOTS + n - 1)
                    dve.tensor_copy(sums[:, n % 2, :], o_bank[n % 2][:]).then_inc(copied, 1)

                def divide(b, n):
                    k = bank_b.next()
                    dve.wait_ge(post.full, k)
                    if not isinstance(b, int) or b * NSLOTS + n > 0:
                        dve.wait_ge(checked, b * NSLOTS + n)
                    dve.reciprocal(recip[:], post.bank[:]).then_inc(post.free, 1)
                    dve.drain()
                    hg, qc = n // NQC, n % NQC
                    dve.tensor_tensor(attn[:, hg, qc * QC:(qc + 1) * QC], sums[:, n % 2, :], recip[:], ALU.mult)\
                       .then_inc(attn_ready, 1)

                def iteration(b, p, q):
                    for s in range(STEPS + 1):
                        if b is not None and s in COPY_AT:
                            copy_sums(b, COPY_AT[s])
                        if p is not None:
                            for kind, k in PREP.get(s, ()):
                                side_item(prep, bank_a, kind, k, p)
                        if q is not None:
                            for kind, k in POST.get(s, ()):
                                side_item(post, bank_b, kind, k, q)
                        if b is not None and s in DENOM_AT:
                            divide(b, DENOM_AT[s])

                dve.wait_ge(weights, 16 * (9 + H))
                dve.wait_ge(tabled, 2)
                for buf in (w_base, half_b):
                    dve.tensor_scalar(buf[:], buf[:], 0.5, None, ALU.mult)
                dve.drain()
                dve.sem_inc(halved, 1)
                dve.sem_inc(prep.free, 1)
                dve.sem_inc(post.free, 1)
                dve.sem_inc(copied, 2)
                if shifted:
                    dve.memset(k_rows[ROWS:n_rows], 1.0).then_inc(ones_ready, 1)
                sequences(dve, iteration, bank_a, bank_b)
                if not shifted:
                    for c in range(2):
                        dve.wait_ge(spread_seen, c + 1)
                        dve.tensor_scalar(sums[:, c, :], o_bank[c][:], (D_LIMIT, INV_D_LIMIT)[c], None, ALU.is_le)
                    dve.drain()
                    for c in range(2):
                        last = dve.tensor_reduce(in_range[:, c:c + 1], sums[:, c, :], AX.X, ALU.min)
                    last.then_inc(in_range_ready, 1)
                    dve.wait_ge(range_summed, 1)
                    dve.tensor_scalar(out_of_range[:, 0:2], prep.bank[:, 0:2], float(P), None, ALU.is_lt)
                    dve.drain()
                    dve.tensor_reduce(out_of_range[:, 2:3], out_of_range[:, 0:2], AX.X, ALU.max)
                    dve.drain()
                    dve.tensor_copy(const["flag"][:, 2:3], out_of_range[:, 2:3])


def build(nc, io):
    with ExitStack() as nc_ctx:
        m = Pools(nc, nc_ctx, "c_")
        const = {
            "ident": m.sb("ident", [P, P]), "ones": m.sb("ones", [P, P]),
            "eps": m.sb("eps", [P, GT]), "minus_half": m.sb("minus_half", [P, GT]),
            "iota0": m.sb("iota0", [P, GT, E0]), "keep": m.sb("keep", [P, 2, E0]), "flag": m.sb("flag", [P, 3], I32),
        }
        built = m.sem("built")
        with nc.Block() as block:
            @block.gpsimd
            def _(pool):
                pool.memset(const["ident"][:], 0.0)
                pool.memset(const["ones"][:], 1.0)
                pool.memset(const["eps"][:], EPS)
                pool.memset(const["minus_half"][:], -0.5)
                pool.drain()
                pool.affine_select(out=const["ident"][:], in_=const["ident"][:], compare_op=ALU.not_equal, fill=1.0,
                                   base=0, pattern=[[-1, P]], channel_multiplier=1)
                pool.iota(const["iota0"][:], pattern=[[0, GT], [1, E0]], base=0, channel_multiplier=0,
                          allow_small_or_imprecise_dtypes=True).then_inc(built, 1)
                pool.wait_ge(built, 1)
        token_pass(nc, io, const, 0, False, io["x"], None, None)
        moe_pass(nc, io, const, 0, io["x"], io["x_moe"])
        token_pass(nc, io, const, 1, True, io["x"], io["x_moe"], io["x_mix"])
        moe_pass(nc, io, const, 1, io["x_mix"], io["x_mix"])
        sequence_pass(nc, io, const, False)
        row_max_pass(nc, io, const)
        sequence_pass(nc, io, const, True)


def _layouts(inp):
    import numpy as np

    c = np.ascontiguousarray

    def rows(a):
        return c(np.broadcast_to(a, (P, a.shape[-1])))

    def column(a):
        return c(a.reshape(-1, P).T)

    def pairs(w):
        return c(w.reshape(H, HD // 2, 2, D).transpose(2, 1, 0, 3).reshape(D, D).T)

    inv_freq = (10000.0 ** (-np.arange(0, HD, 2, dtype=np.float32) / HD)).astype(np.float32)
    angle = np.repeat(inv_freq, H)[:, None] * np.arange(S, dtype=np.float32)[None, :]
    return {
        "x": c(inp["L0_attn_x"].reshape(-1, D)),
        "gate0T": c(inp["L0_ffn_gate_w"].T),
        "w1T": c(inp["L0_ffn_w1"].transpose(0, 2, 1)), "w2T": c(inp["L0_ffn_w2"].transpose(0, 2, 1)),
        "b1": c(inp["L0_ffn_b1"].reshape(E0, DC, P).transpose(2, 0, 1)),
        "b2": c(np.broadcast_to(inp["L0_ffn_b2"], (P, E0, D))),
        "w_inT": c(inp["L0_attn_W_in"].T), "w_g": c(inp["L0_attn_W_g"]), "w_out": c(inp["L0_attn_W_out"]),
        "b_in": column(inp["L0_attn_b_in"]), "b_g": column(inp["L0_attn_b_g"]), "b_sp": column(inp["L0_attn_b_sp"]),
        "b_out": rows(inp["L0_attn_b_out"]), "norm_w": rows(inp["L0_attn_norm_w"]),
        "norm_b": rows(inp["L0_attn_norm_b"]),
        "w_agT": c(np.concatenate([inp["L1_ffn_lora_A"].reshape(NZ, D), inp["L1_ffn_gate_w"]]).T),
        "w_baseT": c(inp["L1_ffn_base_w"].T),
        "w_b": c(inp["L1_ffn_lora_B"].transpose(0, 2, 1).reshape(NZ, D)), "base_b": rows(inp["L1_ffn_base_b"]),
        "w_qT": pairs(inp["L1_attn_Wq"]), "w_kT": pairs(inp["L1_attn_Wk"]),
        "w_vT": c(inp["L1_attn_Wv"].T), "w_oT": c(inp["L1_attn_Wo"].T),
        "cos": np.cos(angle).astype(np.float32), "sin": np.sin(angle).astype(np.float32),
    }


def kernel(**inputs):
    import numpy as np
    import concourse.bacc as bacc
    from concourse.bass_utils import run_bass_kernel_spmd

    inputs = {name: np.asarray(a) for name, a in inputs.items()}
    shape = inputs["L0_attn_x"].shape
    tokens = shape[0] * shape[1]
    arrays = _layouts(inputs)
    nc = bacc.Bacc("TRN2", target_bir_lowering=False, num_devices=1)
    io = {name: nc.dram_tensor(name, a.shape, mybir.dt.from_np(a.dtype), kind="ExternalInput").ap()
          for name, a in arrays.items()}
    io["tokens"] = tokens
    io["cap"] = int(1.25 * tokens / E0)
    for name in ("x_moe", "x_mix"):
        io[name] = nc.dram_tensor(name, (tokens, D), F32).ap()
    io["parts"] = nc.dram_tensor("parts", (shape[0], 2, 3, 2, P, S), BF16).ap()
    io["shift"] = nc.dram_tensor("shift", (shape[0], 3, H, S), BF16).ap()
    io["out"] = nc.dram_tensor("out", (tokens, D), F32, kind="ExternalOutput").ap()
    build(nc, io)
    r = run_bass_kernel_spmd(nc, [arrays], core_ids=[0])
    return r.results[0]["out"].reshape(shape)
```

```python
from contextlib import ExitStack, contextmanager

import concourse.bass as bass
from concourse import mybir

F32 = mybir.dt.float32
BF16 = mybir.dt.bfloat16
U32 = mybir.dt.uint32
I32 = mybir.dt.int32
ACT = mybir.ActivationFunctionType
ALU = mybir.AluOpType
AX = mybir.AxisListType

P = 128
D = 256
DC = D // P
S = 1024
TS = S // P
DIN = 512
FC = DIN // P
E0 = 8
E1 = 10
NT = 8
RANK = 16
NZ = NT * RANK
NZG = NZ + E1
H = 16
HD = 16
HG = 4
NHG = H // HG
QC = 512
NQC = S // QC
KQ = QC // P
GT = 4
GTOK = GT * P
EPS = 1e-5
MASKED = -1e30
D_LIMIT = 1e30
INV_D_LIMIT = 1e25
SLOTS = 6
QPARTS = [0, 0, 0, 1, 1, 2]
KPARTS = [0, 1, 2, 0, 1, 0]
ROWS = SLOTS * HD
RUNS = (((0, 0, 1), (1, 0, 1), (2, 0, 2), (4, 1, 2)), ((0, 0, 3), (3, 0, 2), (5, 0, 1)))
VW = HD + 1
STEPS = NHG * sum(KQ * (qc + 1) for qc in range(NQC))


def at(buf, k):
    if isinstance(k, int):
        return buf[:, k]
    return buf[:, bass.ds(k, 1)].squeeze(1)


def row_bcast(ap, n, shape):
    return ap.unsqueeze(1).to_broadcast(shape)


class Pools:

    def __init__(self, nc, ctx, prefix):
        self.nc, self.ctx, self.prefix, self.sems = nc, ctx, prefix, []

    def sb(self, name, shape, dt=F32):
        return self.ctx.enter_context(self.nc.sbuf_tensor(self.prefix + name, shape, dt))

    def ps(self, name, shape, dt=F32):
        return self.ctx.enter_context(self.nc.psum_tensor(self.prefix + name, shape, dt))

    def sem(self, name):
        self.sems.append(self.nc.alloc_semaphore(self.prefix + name))
        return self.sems[-1]

    def free_sems(self):
        self.nc.all_engine_barrier()
        self.nc.clear_and_free_semaphores(self.sems)
        self.nc.all_engine_barrier()


@contextmanager
def only_if(eng, flag):
    if flag is None:
        yield
    else:
        value = eng.value_load(flag, min_val=0, max_val=1)
        with eng.If(value == 1):
            yield
        with eng.Else():
            eng.nop()
        eng.nop()


def norm_stats(dve, rows, stats, moments):
    for t in range(GT):
        dve.bn_stats(stats[:, t, :], rows(t))
    dve.drain()
    for t in range(GT):
        last = dve.bn_aggr(moments[:, t, :], stats[:, t, :])
    return last


def norm_rstd(pool, moments, var_eps, rstd, eps, minus_half):
    pool.tensor_tensor(var_eps, moments[:, :, 1], eps, ALU.add)
    pool.drain()
    return pool.tensor_tensor(rstd, var_eps, minus_half, ALU.pow)


def norm_apply(dve, out, rows, moments, rstd):
    for t in range(GT):
        last = dve.tensor_scalar(out[:, t, :], rows(t), moments[:, t, 0:1], rstd[:, t:t + 1], ALU.subtract, ALU.mult)
    return last


def token_pass(nc, io, const, stage, mix, src, fallback, dst):
    n_groups = io["tokens"] // GTOK
    pre = f"t{stage}_"
    with ExitStack() as ctx:
        m = Pools(nc, ctx, pre)
        x = m.sb("x", [P, 4, GT, D])
        xT = m.sb("xT", [P, DC, GTOK])
        gate, gate_sum = m.sb("gate", [P, DC, 32]), m.sb("gate_sum", [P, 32])
        logT = m.sb("logT", [P, P])
        logits = m.sb("logits", [P, GT, E0])
        best = m.sb("best", [P, GT, 8])
        best_at = m.sb("best_at", [P, GT, 8], U32)
        chosen0, chosen1 = m.sb("chosen0", [P, GT, E0]), m.sb("chosen1", [P, GT, E0])
        tally = m.sb("tally", [P, GT, E0])
        tally_p = m.sb("tally_p", [P, E0])
        any_keep = m.sb("any_keep", [P, 1])
        psT = [m.ps(f"psT{c}", [P, GTOK]) for c in range(DC)]
        ps_logT = m.ps("ps_logT", [P, GTOK])
        ps_log = m.ps("ps_log", [P, 512])

        loaded, weights, centred = m.sem("loaded"), m.sem("weights"), m.sem("centred")
        gate_zeroed, gate_summed, x_turned, xT_ready = m.sem("gate_zeroed"), m.sem("gate_summed"), m.sem("x_turned"), m.sem("xT_ready")
        logT_ready, logT_copied = m.sem("logT_ready"), m.sem("logT_copied")
        log_ready, group_done, log_waited = m.sem("log_ready"), m.sem("group_done"), m.sem("log_waited")
        tally_ready, summed = m.sem("tally_ready"), m.sem("summed")
        if mix:
            w_inT, w_g = m.sb("w_inT", [P, FC, D]), m.sb("w_g", [P, FC, DIN])
            b_in, b_g, b_sp = m.sb("b_in", [P, FC]), m.sb("b_g", [P, FC]), m.sb("b_sp", [P, FC])
            w_out = m.sb("w_out", [P, FC, D])
            b_out, norm_w, norm_b = m.sb("b_out", [P, D]), m.sb("norm_w", [P, D]), m.sb("norm_b", [P, D])
            w_ig, b_ig, w_so = m.sb("w_ig", [P, DC, DIN]), m.sb("b_ig", [P, FC]), m.sb("w_so", [P, FC, D])
            xn, xnT = m.sb("xn", [P, GT, D]), m.sb("xnT", [P, DC, GTOK])
            xn_b, x_b = m.sb("xn_b", [P, 2, GT, D]), m.sb("x_b", [P, 2, GT, D])
            silu, r, x_out = m.sb("silu", [P, FC, GTOK]), m.sb("r", [P, GT, D]), m.sb("x_out", [P, GT, D])
            stats, moments = m.sb("stats", [P, GT, 6]), m.sb("moments", [P, GT, 2])
            stats2, moments2 = m.sb("stats2", [P, GT, 6]), m.sb("moments2", [P, GT, 2])
            var_eps, rstd = m.sb("var_eps", [P, GT]), m.sb("rstd", [P, GT])
            var_eps2, rstd2 = m.sb("var_eps2", [P, GT]), m.sb("rstd2", [P, GT])
            psG = [m.ps(f"psG{k}", [P, GTOK]) for k in range(2)]
            psY = [m.ps(f"psY{k}", [P, 2, D]) for k in range(2)]
            folded_pe, folded = m.sem("folded_pe"), m.sem("folded")
            moments_ready, rstd_ready, xn_ready = m.sem("moments_ready"), m.sem("rstd_ready"), m.sem("xn_ready")
            turned, xnT_ready = m.sem("turned"), m.sem("xnT_ready")
            shifted_ready, gate_ready, gate_silu = m.sem("shifted_ready"), m.sem("gate_ready"), m.sem("gate_silu")
            mixed, r_ready, x_new = m.sem("mixed"), m.sem("r_ready"), m.sem("x_new")
            moments2_ready, rstd2_ready = m.sem("moments2_ready"), m.sem("rstd2_ready")
            stored = m.sem("stored")

        src_g, dst_g, fb_g = (None if a is None else a.rearrange("(g t p) d -> g p t d", t=GT, p=P)
                              for a in (src, dst, fallback))

        def dram_at(v, g):
            return v[g] if isinstance(g, int) else v[bass.ds(g, 1)].squeeze(0)

        ctx.callback(m.free_sems)
        block = ctx.enter_context(nc.Block())

        @block.sync
        def _(sp):
            def load_from(v):
                def load(g):
                    sp.dma_start(at(x, g % 4), dram_at(v, g)).then_inc(loaded, 16)
                return load

            def run(load):
                def slot_done(g):
                    if mix:
                        sp.wait_ge(x_new, g + 1)
                        sp.dma_start(dram_at(dst_g, g), x_out[:]).then_inc(stored, 16)
                    else:
                        sp.wait_ge(x_turned, (g + 1) * DC)

                for g in range(3):
                    if g:
                        sp.wait_ge(loaded, g * 16)
                    load(g)
                sp.wait_ge(loaded, 48)
                load(3)
                with sp.Fori(0, n_groups - 4) as g:
                    slot_done(g)
                    sp.wait_ge(loaded, g * 16 + 64)
                    load(g + 4)
                for g in range(n_groups - 4, n_groups):
                    slot_done(g)

            sp.wait_ge(gate_zeroed, 1)
            sp.dma_start(gate[:, :, 0:E0], io["gate0T"].rearrange("(c p) e -> p c e", p=P)).then_inc(weights, 16)
            if mix:
                for buf, name in ((w_inT, "w_inT"), (w_g, "w_g"), (w_out, "w_out")):
                    sp.dma_start(buf[:], io[name].rearrange("(c p) e -> p c e", p=P)).then_inc(weights, 16)
                for buf, name in ((b_in, "b_in"), (b_g, "b_g"), (b_sp, "b_sp"), (b_out, "b_out"),
                                  (norm_w, "norm_w"), (norm_b, "norm_b")):
                    sp.dma_start(buf[:], io[name]).then_inc(weights, 16)
            if fallback is None:
                run(load_from(src_g))
            else:
                kept = sp.value_load(const["flag"][0:1, stage - 1:stage], min_val=0, max_val=1)
                with sp.If(kept == 1):
                    run(load_from(fb_g))
                with sp.Else():
                    run(load_from(src_g))
                sp.nop()
            if mix:
                sp.wait_ge(stored, 16 * n_groups)

        n_weights = 16 * (10 if mix else 1)

        @block.tensor
        def _(pe):
            pe.wait_ge(weights, n_weights)
            for c in range(DC):
                last = pe.matmul(ps_logT[:, 0:32], const["ones"][:], gate[:, c, :], start=(c == 0), stop=(c == DC - 1))
            last.then_inc(gate_summed, 1)
            if mix:
                for c in range(DC):
                    for j in range(FC):
                        last = pe.matmul(psG[c][:], w_inT[:, j, c * P:(c + 1) * P], w_g[:, j, :],
                                         start=(j == 0), stop=(j == FC - 1))
                for f in range(FC):
                    for j in range(FC):
                        last = pe.matmul(ps_log[:, f:f + 1], w_g[:, j, f * P:(f + 1) * P], b_in[:, j:j + 1],
                                         start=(j == 0), stop=(j == FC - 1))
                last.then_inc(folded_pe, 1)
                pe.wait_ge(folded, 4)

            pe.wait_ge(centred, 1)

            def turn(tiles, done_sem):
                for c in range(DC):
                    for t in range(GT):
                        last = pe.transpose(psT[c][:, t * P:(t + 1) * P], tiles[:, t, c * P:(c + 1) * P],
                                            const["ident"][:])
                    last.then_inc(done_sem, 1)

            def turn_x(g, slot=None):
                if mix:
                    pe.wait_ge(x_new, g + 1)
                    turn(x_out, x_turned)
                else:
                    pe.wait_ge(loaded, g * 16 + 16)
                    turn(x[:, slot], x_turned)

            def turn_xn(g):
                pe.wait_ge(xn_ready, g + 1)
                turn(xn, turned)

            def log_parts(g):
                pe.wait_ge(xT_ready, (g + 1) * DC)
                for c in range(DC):
                    for t in range(GT):
                        last = pe.matmul(ps_logT[32 * t:32 * t + 32, 0:P], gate[:, c, :], xT[:, c, t * P:(t + 1) * P],
                                         start=(c == 0), stop=(c == DC - 1))
                last.then_inc(logT_ready, 1)

            def log_turn(g):
                pe.wait_ge(logT_copied, g + 1)
                pe.wait_ge(group_done, g + 1)
                pe.sem_inc(log_waited, 1)
                pe.transpose(ps_log[:, 0:P], logT[:], const["ident"][:]).then_inc(log_ready, 1)

            def mix_gate(g):
                pe.wait_ge(xnT_ready, (g + 1) * DC)
                for f in range(FC):
                    pe.wait_ge(gate_silu, g * FC + f + 1)
                    for c in range(DC):
                        last = pe.matmul(psG[f % 2][:], w_ig[:, c, f * P:(f + 1) * P], xnT[:, c, :],
                                         start=(c == 0), stop=(c == DC - 1))
                    last.then_inc(gate_ready, 1)

            def mix_out(g):
                for t in range(GT):
                    if t == 0:
                        pe.wait_ge(gate_silu, (g + 1) * FC + 2)
                    if t % 2 == 0:
                        pe.wait_ge(r_ready, g * 2 + t // 2 + 1)
                    for f in range(FC):
                        last = pe.matmul(psY[t // 2][:, t % 2, :], silu[:, f, t * P:(t + 1) * P], w_so[:, f, :],
                                         start=(f == 0), stop=(f == FC - 1))
                    if t % 2:
                        last.then_inc(mixed, 1)

            if not mix:
                for g in range(4):
                    turn_x(g, g)
                    if g > 0:
                        log_turn(g - 1)
                    log_parts(g)
                with pe.Fori(1, n_groups // 4) as four:
                    for slot in range(4):
                        turn_x(four * 4 + slot, slot)
                        log_turn(four * 4 + slot - 1)
                        log_parts(four * 4 + slot)
                log_turn(n_groups - 1)
            else:
                turn_xn(0)
                mix_gate(0)
                mix_out(0)
                turn_xn(1)
                mix_gate(1)
                turn_x(0)
                mix_out(1)
                with pe.Fori(2, n_groups) as g:
                    pe.wait_ge(xT_ready, (g - 1) * DC)
                    pe.sem_inc(log_waited, 1)
                    turn_xn(g)
                    log_parts(g - 2)
                    mix_gate(g)
                    turn_x(g - 1)
                    log_turn(g - 2)
                    mix_out(g)
                log_parts(n_groups - 2)
                turn_x(n_groups - 1)
                log_turn(n_groups - 2)
                log_parts(n_groups - 1)
                log_turn(n_groups - 1)
            pe.wait_ge(tally_ready, 1)
            pe.matmul(ps_logT[:, 0:E0], const["ones"][:], tally_p[:], start=True, stop=True).then_inc(summed, 1)

        @block.scalar
        def _(act):
            if mix:
                act.wait_ge(folded_pe, 1)
                for c in range(DC):
                    act.activation(w_ig[:, c, :], psG[c][:], ACT.Copy).then_inc(folded, 1)

            def copy_turned(g, done_sem, out, out_ready):
                for c in range(DC):
                    act.wait_ge(done_sem, g * DC + c + 1)
                    act.activation(out[:, c, :], psT[c][:], ACT.Copy).then_inc(out_ready, 1)

            def copy_logT(g):
                act.wait_ge(logT_ready, g + 1)
                act.activation(logT[:], ps_logT[:, 0:P], ACT.Copy).then_inc(logT_copied, 1)

            def silus(g):
                for f in range(FC):
                    act.wait_ge(gate_ready, g * FC + f + 1)
                    act.activation(silu[:, f, :], psG[f % 2][:], ACT.Silu, bias=b_ig[:, f:f + 1]).then_inc(gate_silu, 1)

            if not mix:
                with act.Fori(0, n_groups) as g:
                    copy_turned(g, x_turned, xT, xT_ready)
                    copy_logT(g)
            else:
                act.sem_inc(gate_silu, 2)
                act.wait_ge(folded, 4)
                for g in range(2):
                    copy_turned(g, turned, xnT, xnT_ready)
                    silus(g)
                copy_turned(0, x_turned, xT, xT_ready)
                with act.Fori(2, n_groups) as g:
                    copy_turned(g, turned, xnT, xnT_ready)
                    copy_logT(g - 2)
                    silus(g)
                    copy_turned(g - 1, x_turned, xT, xT_ready)
                copy_logT(n_groups - 2)
                copy_turned(n_groups - 1, x_turned, xT, xT_ready)
                copy_logT(n_groups - 1)

        @block.gpsimd
        def _(pool):
            def rstd_of(g, ready, mom, ve, rs, done_sem):
                pool.wait_ge(ready, g + 1)
                norm_rstd(pool, mom, ve[:], rs[:], const["eps"][:], const["minus_half"][:]).then_inc(done_sem, 1)

            def shifted(g):
                pool.wait_ge(xn_ready, g + 1)
                pool.tensor_tensor(at(xn_b, g % 2), xn[:], row_bcast(b_out[:], GT, [P, GT, D]), ALU.add)
                pool.tensor_tensor(at(x_b, g % 2), at(x, g % 4), row_bcast(norm_b[:], GT, [P, GT, D]),
                                   ALU.add).then_inc(shifted_ready, 1)

            if mix:
                def prepare(g):
                    rstd_of(g, moments_ready, moments, var_eps, rstd, rstd_ready)
                    shifted(g)

                def second(g):
                    rstd_of(g, moments2_ready, moments2, var_eps2, rstd2, rstd2_ready)

                pool.wait_ge(weights, n_weights)
                prepare(0)
                prepare(1)
                with pool.Fori(1, n_groups - 1) as g:
                    second(g - 1)
                    prepare(g + 1)
                second(n_groups - 2)
                second(n_groups - 1)

        @block.vector
        def _(dve):
            dve.memset(gate[:], 0.0).then_inc(gate_zeroed, 1)
            dve.wait_ge(weights, n_weights)
            dve.wait_ge(gate_summed, 1)
            dve.tensor_scalar(gate_sum[:], ps_logT[:, 0:32], 1.0 / D, None, ALU.mult)
            dve.drain()
            dve.tensor_tensor(gate[:], gate[:], row_bcast(gate_sum[:], DC, [P, DC, 32]), ALU.subtract)\
               .then_inc(centred, 1)
            if mix:
                for f in range(FC):
                    last = dve.tensor_scalar(w_so[:, f, :], w_out[:, f, :], b_sp[:, f:f + 1], None, ALU.mult)
                last.then_inc(folded, 1)
                dve.wait_ge(folded_pe, 1)
                dve.tensor_tensor(b_ig[:], ps_log[:, 0:FC], b_g[:], ALU.add).then_inc(folded, 1)
                dve.sem_inc(r_ready, 2)
            dve.memset(tally[:], 0.0)
            dve.sem_inc(group_done, 1)

            def normalise(g):
                dve.wait_ge(loaded, g * 16 + 16)
                rows = lambda t: at(x, g % 4)[:, t, :]
                norm_stats(dve, rows, stats, moments).then_inc(moments_ready, 1)
                dve.wait_ge(rstd_ready, g + 1)
                if not isinstance(g, int) or g > 0:
                    dve.wait_ge(turned, g * DC)
                    if mix:
                        dve.wait_ge(shifted_ready, g)
                norm_apply(dve, xn, rows, moments, rstd).then_inc(xn_ready, 1)

            def mix_sums(g):
                dve.wait_ge(shifted_ready, g + 1)
                for u in range(GT // 2):
                    dve.wait_ge(mixed, g * 2 + u + 1)
                    dve.tensor_tensor(r[:, 2 * u:2 * u + 2, :], psY[u][:], at(xn_b, g % 2)[:, 2 * u:2 * u + 2, :],
                                      ALU.add).then_inc(r_ready, 1)
                dve.drain()
                norm_stats(dve, lambda t: r[:, t, :], stats2, moments2).then_inc(moments2_ready, 1)
                dve.wait_ge(rstd2_ready, g + 1)
                for t in range(GT):
                    dve.tensor_scalar(r[:, t, :], r[:, t, :], moments2[:, t, 0:1], rstd2[:, t:t + 1],
                                      ALU.subtract, ALU.mult)
                dve.drain()
                dve.tensor_tensor(r[:], r[:], row_bcast(norm_w[:], GT, [P, GT, D]), ALU.mult)
                dve.drain()
                if not isinstance(g, int) or g > 0:
                    dve.wait_ge(stored, g * 16)
                    dve.wait_ge(x_turned, g * DC)
                dve.tensor_tensor(x_out[:], r[:], at(x_b, g % 2), ALU.add).then_inc(x_new, 1)

            def route(g):
                dve.wait_ge(log_ready, g + 1)
                dve.tensor_copy(logits[:], ps_log[:, 0:P].rearrange("p (t e) -> p t e", t=GT)[:, :, 0:E0]).then_inc(group_done, 1)
                dve.drain()
                for t in range(GT):
                    dve.max(best[:, t, :], logits[:, t, :])
                dve.drain()
                for t in range(GT):
                    dve.max_index(best_at[:, t, :], best[:, t, :], logits[:, t, :])
                dve.drain()
                for k, chosen in ((0, chosen0), (1, chosen1)):
                    dve.tensor_tensor(chosen[:], const["iota0"][:], best_at[:, :, k:k + 1].to_broadcast([P, GT, E0]),
                                      ALU.is_equal)
                dve.drain()
                dve.tensor_tensor(tally[:], tally[:], chosen0[:], ALU.add)
                dve.drain()
                dve.tensor_tensor(tally[:], tally[:], chosen1[:], ALU.add)

            if not mix:
                with dve.Fori(0, n_groups) as g:
                    route(g)
            else:
                normalise(0)
                normalise(1)
                mix_sums(0)
                normalise(2)
                with dve.Fori(2, n_groups - 1) as g:
                    mix_sums(g - 1)
                    normalise(g + 1)
                    route(g - 2)
                mix_sums(n_groups - 2)
                route(n_groups - 3)
                mix_sums(n_groups - 1)
                route(n_groups - 2)
                route(n_groups - 1)
            dve.drain()
            dve.tensor_reduce(tally_p[:], tally[:].rearrange("p t e -> p e t"), AX.X, ALU.add).then_inc(tally_ready, 1)
            dve.wait_ge(summed, 1)
            keep = const["keep"][:, stage, :]
            dve.tensor_scalar(keep, ps_logT[:, 0:E0], float(io["cap"]), None, ALU.is_le)
            dve.drain()
            dve.tensor_reduce(any_keep[:], keep, AX.X, ALU.max)
            dve.drain()
            dve.tensor_copy(const["flag"][:, stage:stage + 1], any_keep[:])



def moe_pass(nc, io, const, stage, src, dst):
    n_groups = io["tokens"] // GTOK
    with ExitStack() as ctx:
        m = Pools(nc, ctx, f"e{stage}_")
        x, xn, xnT = m.sb("x", [P, GT, D]), m.sb("xn", [P, GT, D]), m.sb("xnT", [P, DC, GTOK])
        stats, moments = m.sb("stats", [P, GT, 6]), m.sb("moments", [P, GT, 2])
        var_eps, rstd = m.sb("var_eps", [P, GT]), m.sb("rstd", [P, GT])
        gate = m.sb("gate", [P, DC, E0])
        w1, w2 = m.sb("w1", [P, E0, DC, D]), m.sb("w2", [P, E0, DC, D])
        b1, b2 = m.sb("b1", [P, E0, DC]), m.sb("b2", [P, E0, D])
        logits, share = m.sb("logits", [P, GT, E0]), m.sb("share", [P, GT, E0])
        best, best_at = m.sb("best", [P, GT, 8]), m.sb("best_at", [P, GT, 8], U32)
        chosen0, chosen1 = m.sb("chosen0", [P, GT, E0]), m.sb("chosen1", [P, GT, E0])
        total, inv_total = m.sb("total", [P, GT]), m.sb("inv_total", [P, GT])
        hidden, y = m.sb("hidden", [P, DC, GTOK]), m.sb("y", [P, 2, D])
        psT = [m.ps(f"psT{c}", [P, GTOK]) for c in range(DC)]
        psH = [m.ps(f"psH{c}", [P, GTOK]) for c in range(DC)]
        psY = [m.ps(f"psY{u}", [P, 2, D]) for u in range(2)]
        ps_log = m.ps("ps_log", [P, 512])
        weights, loaded, stored = m.sem("weights"), m.sem("loaded"), m.sem("stored")
        slot_waited = m.sem("slot_waited")
        moments_ready, rstd_ready, xn_ready = m.sem("moments_ready"), m.sem("rstd_ready"), m.sem("xn_ready")
        turned, xnT_ready, log_ready = m.sem("turned"), m.sem("xnT_ready"), m.sem("log_ready")
        gap_ready, exp_ready = m.sem("gap_ready"), m.sem("exp_ready")
        hidden_made, silu_made = m.sem("hidden_made"), m.sem("silu_made")
        y_made, y_taken, x_new = m.sem("y_made"), m.sem("y_taken"), m.sem("x_new")
        src_g, dst_g = (a.rearrange("(g t p) d -> g p t d", t=GT, p=P) for a in (src, dst))
        flag = const["flag"][0:1, stage:stage + 1]
        ctx.callback(m.free_sems)
        block = ctx.enter_context(nc.Block())

        @block.sync
        def _(sp):
            with only_if(sp, flag):
                sp.dma_start(gate[:], io["gate0T"].rearrange("(c p) e -> p c e", p=P)).then_inc(weights, 16)
                sp.dma_start(w1[:], io["w1T"].rearrange("e (c p) f -> p e c f", p=P)).then_inc(weights, 16)
                sp.dma_start(w2[:], io["w2T"].rearrange("e (c p) f -> p e c f", p=P)).then_inc(weights, 16)
                sp.dma_start(b1[:], io["b1"]).then_inc(weights, 16)
                sp.dma_start(b2[:], io["b2"]).then_inc(weights, 16)
                with sp.Fori(0, n_groups) as g:
                    sp.dma_start(x[:], src_g[bass.ds(g, 1)].squeeze(0)).then_inc(loaded, 16)
                    sp.wait_ge(x_new, g + 1)
                    sp.dma_start(dst_g[bass.ds(g, 1)].squeeze(0), x[:]).then_inc(stored, 16)
                    sp.wait_ge(stored, g * 16 + 16)
                    sp.sem_inc(slot_waited, 1)

        @block.tensor
        def _(pe):
            with only_if(pe, flag):
                pe.wait_ge(weights, 80)
                with pe.Fori(0, n_groups) as g:
                    pe.wait_ge(xn_ready, g + 1)
                    for c in range(DC):
                        for t in range(GT):
                            last = pe.transpose(psT[c][:, t * P:(t + 1) * P], xn[:, t, c * P:(c + 1) * P],
                                                const["ident"][:])
                        last.then_inc(turned, 1)
                    pe.wait_ge(xnT_ready, g * DC + DC)
                    for t in range(GT):
                        for c in range(DC):
                            last = pe.matmul(ps_log[:, t * E0:(t + 1) * E0], xnT[:, c, t * P:(t + 1) * P],
                                             gate[:, c, :], start=(c == 0), stop=(c == DC - 1))
                    last.then_inc(log_ready, 1)
                    for e in range(E0):
                        n = g * (E0 * 2) + e * 2
                        for f in range(DC):
                            pe.wait_ge(silu_made, n + f + 1)
                            for c in range(DC):
                                last = pe.matmul(psH[f][:], w1[:, e, c, f * P:(f + 1) * P], xnT[:, c, :],
                                                 start=(c == 0), stop=(c == DC - 1))
                            last.then_inc(hidden_made, 1)
                        pe.wait_ge(silu_made, n + 4)
                        for u in range(2):
                            pe.wait_ge(y_taken, n + u + 1)
                            for t in range(2):
                                tok = slice((2 * u + t) * P, (2 * u + t + 1) * P)
                                for f in range(DC):
                                    last = pe.matmul(psY[u][:, t, :], hidden[:, f, tok], w2[:, e, f, :],
                                                     start=(f == 0), stop=(f == DC - 1))
                            last.then_inc(y_made, 1)

        @block.scalar
        def _(act):
            with only_if(act, flag):
                act.sem_inc(silu_made, 2)
                act.wait_ge(weights, 80)
                with act.Fori(0, n_groups) as g:
                    for c in range(DC):
                        act.wait_ge(turned, g * DC + c + 1)
                        act.activation(xnT[:, c, :], psT[c][:], ACT.Copy).then_inc(xnT_ready, 1)
                    act.wait_ge(gap_ready, g + 1)
                    act.activation(share[:], share[:], ACT.Exp).then_inc(exp_ready, 1)
                    for e in range(E0):
                        n = g * (E0 * 2) + e * 2
                        act.wait_ge(y_taken, n + 2)
                        for f in range(DC):
                            act.wait_ge(hidden_made, n + f + 1)
                            act.activation(hidden[:, f, :], psH[f][:], ACT.Silu, bias=b1[:, e, f:f + 1])\
                               .then_inc(silu_made, 1)

        @block.gpsimd
        def _(pool):
            with only_if(pool, flag):
                with pool.Fori(0, n_groups) as g:
                    pool.wait_ge(moments_ready, g + 1)
                    norm_rstd(pool, moments, var_eps[:], rstd[:], const["eps"][:],
                              const["minus_half"][:]).then_inc(rstd_ready, 1)

        @block.vector
        def _(dve):
            with only_if(dve, flag):
                dve.sem_inc(y_taken, 2)
                dve.wait_ge(weights, 80)
                with dve.Fori(0, n_groups) as g:
                    rows = lambda t: x[:, t, :]
                    dve.wait_ge(loaded, g * 16 + 16)
                    norm_stats(dve, rows, stats, moments).then_inc(moments_ready, 1)
                    dve.wait_ge(rstd_ready, g + 1)
                    norm_apply(dve, xn, rows, moments, rstd).then_inc(xn_ready, 1)
                    dve.wait_ge(log_ready, g + 1)
                    dve.tensor_copy(logits[:], ps_log[:, 0:GT * E0])
                    dve.drain()
                    for t in range(GT):
                        dve.max(best[:, t, :], logits[:, t, :])
                    dve.drain()
                    for t in range(GT):
                        dve.max_index(best_at[:, t, :], best[:, t, :], logits[:, t, :])
                    dve.tensor_tensor(share[:], logits[:], best[:, :, 0:1].to_broadcast([P, GT, E0]), ALU.subtract)\
                       .then_inc(gap_ready, 1)
                    dve.drain()
                    for k, chosen in ((0, chosen0), (1, chosen1)):
                        dve.tensor_tensor(chosen[:], const["iota0"][:],
                                          best_at[:, :, k:k + 1].to_broadcast([P, GT, E0]), ALU.is_equal)
                    dve.drain()
                    dve.tensor_tensor(chosen0[:], chosen0[:], chosen1[:], ALU.add)
                    dve.drain()
                    dve.tensor_tensor(chosen0[:], chosen0[:],
                                      row_bcast(const["keep"][:, stage, :], GT, [P, GT, E0]), ALU.mult)
                    dve.wait_ge(exp_ready, g + 1)
                    dve.tensor_reduce(total[:], share[:], AX.X, ALU.add)
                    dve.drain()
                    dve.tensor_tensor(share[:], share[:], chosen0[:], ALU.mult)
                    dve.reciprocal(inv_total[:], total[:])
                    dve.drain()
                    dve.tensor_scalar(inv_total[:], inv_total[:], 0.5, None, ALU.mult)
                    dve.drain()
                    dve.tensor_tensor(share[:], share[:], inv_total[:].unsqueeze(2).to_broadcast([P, GT, E0]),
                                      ALU.mult)
                    for e in range(E0):
                        for u in range(2):
                            dve.wait_ge(y_made, g * (E0 * 2) + e * 2 + u + 1)
                            dve.tensor_tensor(y[:], psY[u][:], row_bcast(b2[:, e, :], 2, [P, 2, D]), ALU.add)\
                               .then_inc(y_taken, 1)
                            dve.drain()
                            for t in range(2):
                                dve.tensor_scalar(y[:, t, :], y[:, t, :], share[:, 2 * u + t, e:e + 1], None, ALU.mult)
                            dve.drain()
                            last = dve.tensor_tensor(x[:, 2 * u:2 * u + 2, :], x[:, 2 * u:2 * u + 2, :], y[:], ALU.add)
                            if e == E0 - 1 and u == 1:
                                last.then_inc(x_new, 1)
                            else:
                                dve.drain()


TAIL = STEPS
PREP = {
    2: [("stats", 0)], 3: [("stats", 1), ("norm", 0)], 4: [("turn", 0)], 5: [("turn", 1)], 6: [("norm", 1)],
    8: [("turn", 2)], 9: [("turn", 3)], 10: [("zg", 0)], 11: [("zg", 1), ("bias", 0)], 12: [("zg", 2)],
    13: [("zg", 3)], 14: [("route", 0)], 16: [("gate_exp", 0)], 17: [("weigh", 0)], 18: [("zturn", 0)],
    19: [("zturn", 1)], 20: [("y", 0)], 21: [("y", 1)], 22: [("y", 2), ("stats", 2)], 23: [("y", 3), ("norm", 2)],
    24: [("stats", 3)], 25: [("turn", 4)], 26: [("turn", 5), ("norm", 3)], 28: [("turn", 6)], 29: [("turn", 7)],
    30: [("qk", 0)], 31: [("qk", 1)], 32: [("high", 0)], 33: [("qk", 2), ("mid", 0)], 34: [("qk", 3), ("low", 0)],
    35: [("high", 1)], 36: [("qk", 4), ("mid", 1)], 37: [("qk", 5), ("low", 1)],
    38: [("high", 2), ("qk", 6), ("mid", 2)], 39: [("qk", 7), ("low", 2)], 41: [("high", 3)], 42: [("mid", 3)],
    43: [("low", 3), ("v", 0)], 45: [("v", 1)], 47: [("v", 2)], TAIL: [("v", 3)],
}
POST = {
    1: [("wo", 0)], 2: [("wo", 1)], 3: [("wo", 2), ("stats", 0)], 4: [("wo", 3)], 5: [("stats", 1), ("norm", 0)],
    8: [("turn", 0)], 9: [("turn", 1)], 10: [("norm", 1)], 12: [("turn", 2)], 13: [("turn", 3)], 15: [("bias", 0)],
    16: [("zg", 0)], 17: [("zg", 1)], 20: [("zg", 2)], 21: [("zg", 3)], 22: [("route", 0)], 24: [("gate_exp", 0)],
    25: [("weigh", 0)], 32: [("zturn", 0)], 33: [("zturn", 1)], 34: [("y", 0)], 35: [("y", 1)], 37: [("y", 2)],
    40: [("y", 3)], 43: [("store", 0)],
}
BANKED = {"turn", "zg", "zturn", "y", "qk", "v", "wo", "denom"}
SLOT_OF, SLOT_END = [], []
for _hg in range(NHG):
    for _qc in range(NQC):
        SLOT_OF += [(_hg, _qc, _kb) for _kb in range(KQ * (_qc + 1))]
        SLOT_END.append(len(SLOT_OF) - 1)
NSLOTS = len(SLOT_END)
HGSTEPS = STEPS // NHG
COPY_AT = {min(e + 1, TAIL): n for n, e in enumerate(SLOT_END)}
DENOM_AT = {min(e + 3, TAIL): n for n, e in enumerate(SLOT_END)}


def banked(table):
    return sum(kind in BANKED for items in table.values() for kind, _ in items)


N_PREP, N_POST = banked(PREP), banked(POST)


class Uses:

    def __init__(self):
        self.base, self.k = 0, 0

    def next(self):
        self.k += 1
        return self.base + self.k

    def so_far(self):
        return self.base + self.k

    def enter(self, turns, per_turn):
        self.start = self.base + self.k
        self.base, self.k = turns * per_turn + self.start, 0

    def leave(self, turns, per_turn):
        self.base, self.k = self.start + turns * per_turn, 0


def row_max_pass(nc, io, const):
    NB = io["tokens"] // S
    with ExitStack() as ctx:
        m = Pools(nc, ctx, "m_")
        q_rows, k_rows = m.sb("q_rows", [ROWS, HG, S], BF16), m.sb("k_rows", [ROWS, HG, S], BF16)
        identb, mask = m.sb("identb", [P, P], BF16), m.sb("mask", [P, P], BF16)
        row_max, row_maxT = m.sb("row_max", [P, HG * TS]), m.sb("row_maxT", [HG * TS, P])
        rest, part = m.sb("rest", [HG * TS, P]), m.sb("part", [HG * TS, 3, P], BF16)
        s_tile = [m.ps(f"s_tile{k}", [P, S]) for k in range(2)]
        turned = m.ps("turned", [P, QC])
        rows_loaded, part_stored, tabled = m.sem("rows_loaded"), m.sem("part_stored"), m.sem("tabled")
        scored, maxed, max_ready = m.sem("scored"), m.sem("maxed"), m.sem("max_ready")
        max_turned, part_ready, waited = m.sem("max_turned"), m.sem("part_ready"), m.sem("waited")
        parts_r = io["parts"].rearrange("b a c e (i g j) t -> b g a (c e i) (j t)", g=NHG, j=HG)
        shift_w = io["shift"].rearrange("b c (g j) (u p) -> b g (j u) c p", j=HG, p=P)
        flag = const["flag"][0:1, 2:3]
        NSC = HG * TS
        ctx.callback(m.free_sems)
        block = ctx.enter_context(nc.Block())

        @block.sync
        def _(sp):
            with only_if(sp, flag):
                with sp.Fori(0, NB) as b:
                    for hg in range(NHG):
                        src = parts_r[bass.ds(b, 1)].squeeze(0)[hg]
                        for a, buf in ((0, q_rows), (1, k_rows)):
                            for slot, c, n in RUNS[a]:
                                sp.dma_start(buf[slot * HD:(slot + n) * HD].rearrange("r h t -> r (h t)"),
                                             src[a, c * HD:(c + n) * HD]).then_inc(rows_loaded, 16)
                        sp.wait_ge(part_ready, b * NHG + hg + 1)
                        for c in range(3):
                            sp.dma_start(shift_w[bass.ds(b, 1)].squeeze(0)[hg, :, c], part[:, c, :])\
                              .then_inc(part_stored, 16)
                        sp.wait_ge(part_stored, (b * NHG + hg) * 48 + 48)
                        sp.sem_inc(waited, 1)

        @block.gpsimd
        def _(pool):
            with only_if(pool, flag):
                pool.memset(identb[:], 0.0)
                pool.memset(mask[:], 0.0)
                pool.drain()
                pool.affine_select(out=identb[:], in_=identb[:], compare_op=ALU.not_equal, fill=1.0,
                                   base=0, pattern=[[-1, P]], channel_multiplier=1)
                pool.affine_select(out=mask[:], in_=mask[:], compare_op=ALU.is_ge, fill=MASKED,
                                   base=0, pattern=[[-1, P]], channel_multiplier=1)
                pool.drain()
                pool.sem_inc(tabled, 1)

        @block.tensor
        def _(pe):
            with only_if(pe, flag):
                pe.wait_ge(tabled, 1)
                with pe.Fori(0, NB) as b:
                    for hg in range(NHG):
                        base = (b * NHG + hg) * NSC
                        pe.wait_ge(rows_loaded, (b * NHG + hg) * 112 + 112)
                        for n in range(NSC):
                            h, qt = n // TS, n % TS
                            tile = s_tile[n % 2]
                            if n >= 2:
                                pe.wait_ge(maxed, base + n - 1)
                            for k0 in range(0, (qt + 1) * P, QC):
                                k1 = min(k0 + QC, (qt + 1) * P)
                                pe.matmul(tile[:, k0:k1], q_rows[:, h, qt * P:(qt + 1) * P], k_rows[:, h, k0:k1],
                                          start=True, stop=True)
                            pe.matmul(tile[:, qt * P:(qt + 1) * P], identb[:], mask[:], start=False, stop=True,
                                      skip_group_check=True).then_inc(scored, 1)
                        pe.wait_ge(max_ready, b * NHG + hg + 1)
                        pe.transpose(turned[0:NSC, 0:P], row_max[:], const["ident"][:]).then_inc(max_turned, 1)

        @block.vector
        def _(dve):
            with only_if(dve, flag):
                with dve.Fori(0, NB) as b:
                    for hg in range(NHG):
                        base = (b * NHG + hg) * NSC
                        for n in range(NSC):
                            qt = n % TS
                            dve.wait_ge(scored, base + n + 1)
                            dve.tensor_reduce(row_max[:, n:n + 1], s_tile[n % 2][:, 0:(qt + 1) * P], AX.X, ALU.max)\
                               .then_inc(maxed, 1)
                        dve.drain()
                        dve.sem_inc(max_ready, 1)
                        dve.wait_ge(max_turned, b * NHG + hg + 1)
                        dve.tensor_scalar(row_maxT[:], turned[0:NSC, 0:P], -1.0, None, ALU.mult)
                        dve.drain()
                        dve.tensor_copy(part[:, 0, :], row_maxT[:])
                        dve.drain()
                        dve.tensor_tensor(rest[:], row_maxT[:], part[:, 0, :], ALU.subtract)
                        dve.drain()
                        dve.tensor_copy(part[:, 1, :], rest[:])
                        dve.drain()
                        dve.tensor_tensor(part[:, 2, :], rest[:], part[:, 1, :], ALU.subtract).then_inc(part_ready, 1)


def sequence_pass(nc, io, const, shifted):
    NB = io["tokens"] // S
    n_rows = ROWS + (3 if shifted else 0)
    per_rows = 16 * (8 if shifted else 7)
    flag = const["flag"][0:1, 2:3] if shifted else None
    with ExitStack() as ctx:
        m = Pools(nc, ctx, "r_" if shifted else "s_")
        x = m.sb("x", [P, 3, TS, D])
        w_ag, w_base, w_b = m.sb("w_ag", [P, DC, NZG]), m.sb("w_base", [P, DC, D]), m.sb("w_b", [P, D])
        half_b = m.sb("half_b", [P, D])
        w_qk = m.sb("w_qk", [P, 2, DC, D])
        w_v, w_o = m.sb("w_v", [P, DC, D]), m.sb("w_o", [P, NHG // 2, D])
        halves = m.sb("halves", [P, 2])
        cos, sin = m.sb("cos", [P, S]), m.sb("sin", [P, S])
        identb, mask = m.sb("identb", [P, P], BF16), m.sb("mask", [P, P], BF16)
        spread = m.sb("spread", [P, 2, P])
        q_rows, k_rows = m.sb("q_rows", [n_rows, 2, HG, S], BF16), m.sb("k_rows", [n_rows, 2, HG, S], BF16)
        v = m.sb("v", [P, TS * H * VW + 16])
        v_heads = v[:, 0:TS * H * VW].rearrange("p (t h w) -> p t h w", t=TS, w=VW)
        probs = m.sb("probs", [P, 2, HG, QC])
        sums, recip = m.sb("sums", [P, 2, QC]), m.sb("recip", [P, QC])
        attn, attn_odd = m.sb("attn", [P, NHG // 2, S]), m.sb("attn_odd", [P, QC])
        rope = m.sb("rope", [P, 4, QC])
        turned_qk, rest = m.sb("turned_qk", [P, 2, QC]), m.sb("rest", [P, 2, QC])
        part = [m.sb(f"part{c}", [P, 2, QC], BF16) for c in range(3)]
        seen = m.sb("seen", [P, 2, 2, QC])
        iota = m.sb("iota", [P, NT])

        s_tile = [m.ps(f"s_tile{p}", [P, 2, QC]) for p in range(2)]
        o_bank = [m.ps(f"o_bank{p}", [P, QC]) for p in range(2)]

        class Side:

            def __init__(self, name, norms):
                self.norms = norms
                self.xn, self.xnT = m.sb(name + "xn", [P, GT, D]), m.sb(name + "xnT", [P, DC, S])
                self.stats = [m.sb(f"{name}stats{g}", [P, GT, 6]) for g in range(2)]
                self.moments = [m.sb(f"{name}moments{g}", [P, GT, 2]) for g in range(2)]
                self.var_eps, self.rstd = m.sb(name + "var_eps", [P, 2, GT]), m.sb(name + "rstd", [P, 2, GT])
                self.zg, self.zT = m.sb(name + "zg", [P, TS, NZG]), m.sb(name + "zT", [P, S])
                self.best, self.best_at = m.sb(name + "best", [P, TS, 8]), m.sb(name + "best_at", [P, TS, 8], U32)
                self.c0, self.c1 = m.sb(name + "c0", [P, TS, NT]), m.sb(name + "c1", [P, TS, NT])
                self.gap, self.den = m.sb(name + "gap", [P, TS, NT]), m.sb(name + "den", [P, 3, TS])
                self.bank = m.ps(name + "bank", [P, QC])
                self.full, self.free = m.sem(name + "full"), m.sem(name + "free")
                self.moments_ready, self.rstd_ready = m.sem(name + "moments_ready"), m.sem(name + "rstd_ready")
                self.xn_ready = m.sem(name + "xn_ready")
                self.biased, self.gap_ready = m.sem(name + "biased"), m.sem(name + "gap_ready")
                self.exp_ready, self.z_ready = m.sem(name + "exp_ready"), m.sem(name + "z_ready")

        prep, post = Side("prep_", 4), Side("post_", 2)
        weights, tabled, halved = m.sem("weights"), m.sem("tabled"), m.sem("halved")
        x_loaded, x_stored = m.sem("x_loaded"), m.sem("x_stored")
        scored = [m.sem(f"scored{p}") for p in range(2)]
        exped = [m.sem(f"exped{p}") for p in range(2)]
        used, copied = m.sem("used"), m.sem("copied")
        checked, rotated, attn_ready = m.sem("checked"), m.sem("rotated"), m.sem("attn_ready")
        part_ready = [m.sem(f"part_ready{c}") for c in range(3)]
        part_stored = [m.sem(f"part_stored{c}") for c in range(3)]
        rest_ready = m.sem("rest_ready")
        rows_loaded = [m.sem(f"rows_loaded{k}") for k in range(2)]
        in_range, out_of_range = m.sb("in_range", [P, 4]), m.sb("out_of_range", [P, 5])
        seen_ready, spread_seen, ones_ready = m.sem("seen_ready"), m.sem("spread_seen"), m.sem("ones_ready")
        in_range_ready, range_summed = m.sem("in_range_ready"), m.sem("range_summed")

        x_in = io["x_mix"].rearrange("(b t p) d -> b p t d", t=TS, p=P)
        x_out = io["out"].rearrange("(b t p) d -> b p t d", t=TS, p=P)
        parts_w = io["parts"].rearrange("b a c e r t -> b a c r e t")
        parts_r = io["parts"].rearrange("b a c e (i h) t -> b a (c e i) (h t)", h=H)

        def dram_at(vw, b):
            return vw[b] if isinstance(b, int) else vw[bass.ds(b, 1)].squeeze(0)

        def sequences(eng, iteration, uses_a, uses_b):
            iteration(None, 0, None)
            iteration(0, 1, None)
            with eng.Fori(1, NB - 1) as b:
                uses_a.enter(b - 1, N_PREP)
                uses_b.enter(b - 1, N_POST + NSLOTS)
                iteration(b, b + 1, b - 1)
            uses_a.leave(NB - 2, N_PREP)
            uses_b.leave(NB - 2, N_POST + NSLOTS)
            iteration(NB - 1, None, NB - 2)
            iteration(None, None, NB - 1)

        ctx.callback(m.free_sems)
        block = ctx.enter_context(nc.Block())

        @block.sync
        def _(sp):
            with only_if(sp, flag):
                bank_b = Uses()
                sp.sem_inc(x_stored, 16)
                for buf, name in ((w_ag, "w_agT"), (w_base, "w_baseT"), (w_v, "w_vT"), (w_o, "w_oT")):
                    sp.dma_start(buf[:], io[name].rearrange("(c p) e -> p c e", p=P)).then_inc(weights, 16)
                sp.dma_start(w_qk[:, 0], io["w_qT"].rearrange("(c p) e -> p c e", p=P)).then_inc(weights, 16)
                sp.dma_start(w_qk[:, 1], io["w_kT"].rearrange("(c p) e -> p c e", p=P)).then_inc(weights, 16)
                for buf, name in ((w_b, "w_b"), (half_b, "base_b"), (cos, "cos"), (sin, "sin"), (halves, "halves")):
                    sp.dma_start(buf[:], io[name]).then_inc(weights, 16)

                def rows(b, hg):
                    k = hg % 2
                    if not (isinstance(b, int) and b == 0 and hg < 2):
                        sp.wait_ge(used, b * STEPS + HGSTEPS * (hg - 1) + 2)
                    span = slice(hg * HG * S, (hg + 1) * HG * S)
                    for a, buf in ((0, q_rows), (1, k_rows)):
                        for slot, c, n in RUNS[a]:
                            sp.dma_start(buf[slot * HD:(slot + n) * HD, k, :, :].rearrange("r h t -> r (h t)"),
                                         dram_at(parts_r, b)[a, c * HD:(c + n) * HD, span]).then_inc(rows_loaded[k], 16)
                    if shifted:
                        sp.dma_start(q_rows[ROWS:n_rows, k], dram_at(io["shift"], b)[:, hg * HG:(hg + 1) * HG, :])\
                          .then_inc(rows_loaded[k], 16)

                def store_part(b, j, c):
                    a, g = j % 2, j // 2
                    sp.wait_ge(part_ready[c], b * 4 + j + 1)
                    sp.dma_start(dram_at(parts_w, b)[a, c, :, :, g * QC:(g + 1) * QC], part[c][:]).then_inc(part_stored[c], 16)

                def iteration(b, p, q):
                    for s in range(STEPS + 1):
                        if s == 0 and p is not None:
                            if not isinstance(p, int) or p >= 3:
                                sp.wait_ge(x_stored, (p - 1) * 16)
                            sp.dma_start(at(x, p % 3), dram_at(x_in, p)).then_inc(x_loaded, 16)
                        if b is not None and s in (HGSTEPS, 2 * HGSTEPS):
                            rows(b, s // HGSTEPS + 1)
                        if p is not None:
                            for kind, j in PREP.get(s, ()):
                                if kind == "high":
                                    store_part(p, j, 0)
                                if kind == "mid":
                                    store_part(p, j, 1)
                                if kind == "low":
                                    store_part(p, j, 2)
                                    if j == 3:
                                        for c in range(3):
                                            sp.wait_ge(part_stored[c], p * 64 + 64)
                                        rows(p, 0)
                        if q is not None:
                            for kind, _ in POST.get(s, ()):
                                if kind in BANKED:
                                    bank_b.next()
                                if kind == "store":
                                    sp.wait_ge(post.free, bank_b.so_far() + 1)
                                    sp.dma_start(dram_at(x_out, q), at(x, q % 3)).then_inc(x_stored, 16)
                        if b is not None and s in DENOM_AT:
                            bank_b.next()
                    if p is not None:
                        rows(p, 1)

                sequences(sp, iteration, Uses(), bank_b)
                sp.wait_ge(x_stored, 16 * NB + 16)

        @block.tensor
        def _(pe):
            with only_if(pe, flag):
                bank_a, bank_b = Uses(), Uses()

                def fill(side, uses):
                    n = uses.next()
                    pe.wait_ge(side.free, n)

                def side_item(side, uses, kind, k, b):
                    if kind in BANKED:
                        fill(side, uses)
                    if kind == "turn":
                        g, c = k // 2, k % 2
                        pe.wait_ge(side.xn_ready, b * side.norms + g + 1)
                        for t in range(GT):
                            last = pe.transpose(side.bank[:, t * P:(t + 1) * P], side.xn[:, t, c * P:(c + 1) * P],
                                                const["ident"][:])
                        last.then_inc(side.full, 1)
                    if kind == "zg":
                        for t in range(2):
                            for c in range(DC):
                                last = pe.matmul(side.bank[:, t * NZG:(t + 1) * NZG],
                                                 side.xnT[:, c, (2 * k + t) * P:(2 * k + t + 1) * P], w_ag[:, c, :],
                                                 start=(c == 0), stop=(c == DC - 1))
                        last.then_inc(side.full, 1)
                    if kind == "zturn":
                        pe.wait_ge(side.z_ready, b + 1)
                        for t in range(GT):
                            last = pe.transpose(side.bank[:, t * P:(t + 1) * P], side.zg[:, GT * k + t, 0:NZ],
                                                const["ident"][:])
                        last.then_inc(side.full, 1)
                    if kind == "y":
                        for t in range(2):
                            tok = slice((2 * k + t) * P, (2 * k + t + 1) * P)
                            for c in range(DC):
                                pe.matmul(side.bank[:, t * D:(t + 1) * D], side.xnT[:, c, tok], w_base[:, c, :],
                                          start=(c == 0), stop=False)
                            last = pe.matmul(side.bank[:, t * D:(t + 1) * D], side.zT[:, tok], w_b[:],
                                             start=False, stop=True)
                        last.then_inc(side.full, 1)
                    if kind == "qk":
                        j, eo = k // 2, k % 2
                        a, g = j % 2, j // 2
                        for c in range(DC):
                            last = pe.matmul(side.bank[:], w_qk[:, a, c, eo * P:(eo + 1) * P],
                                             side.xnT[:, c, g * QC:(g + 1) * QC], start=(c == 0), stop=(c == DC - 1))
                        last.then_inc(side.full, 1)
                    if kind == "v":
                        for t in range(2):
                            for c in range(DC):
                                last = pe.matmul(side.bank[:, t * D:(t + 1) * D],
                                                 side.xnT[:, c, (2 * k + t) * P:(2 * k + t + 1) * P], w_v[:, c, :],
                                                 start=(c == 0), stop=(c == DC - 1))
                        last.then_inc(side.full, 1)
                    if kind == "wo":
                        pe.wait_ge(attn_ready, b * NSLOTS + NSLOTS)
                        for t in range(2):
                            for c in range(NHG // 2):
                                last = pe.matmul(side.bank[:, t * D:(t + 1) * D],
                                                 attn[:, c, (2 * k + t) * P:(2 * k + t + 1) * P], w_o[:, c, :],
                                                 start=(c == 0), stop=(c == NHG // 2 - 1))
                        last.then_inc(side.full, 1)

                def score(b, s):
                    hg, qc, kb = SLOT_OF[s]
                    off = max(kb - KQ * qc, 0) * P
                    if s % HGSTEPS == 0:
                        pe.wait_ge(rows_loaded[hg % 2], (b * 2 + hg // 2 + 1) * per_rows)
                    for p in range(2):
                        pe.wait_ge(exped[p], b * STEPS + s + 1)
                        for j in range(2):
                            h = 2 * p + j
                            last = pe.matmul(s_tile[p][:, j, off:QC], k_rows[:, hg % 2, h, kb * P:(kb + 1) * P],
                                             q_rows[:, hg % 2, h, qc * QC + off:(qc + 1) * QC],
                                             start=True, stop=True)
                            if kb >= KQ * qc:
                                last = pe.matmul(s_tile[p][:, j, off:off + P], mask[:], identb[:],
                                                 start=False, stop=True, skip_group_check=True)
                        last.then_inc(scored[p], 1)

                def weigh_v(b, s):
                    hg, qc, kb = SLOT_OF[s]
                    n = hg * NQC + qc
                    off = max(kb - KQ * qc, 0) * P
                    if s == 0:
                        pe.wait_ge(prep.free, bank_a.so_far() + 1)
                    if kb == 0:
                        pe.wait_ge(copied, b * NSLOTS + n + 1)
                    for p in range(2):
                        pe.wait_ge(exped[p], b * STEPS + s + 2)
                    for h in range(HG):
                        col = (kb * H + hg * HG + h) * VW - HD * (hg % 2)
                        last = pe.matmul(o_bank[n % 2][32 * h:32 * h + 32, off:QC], v[:, col:col + 32],
                                         probs[:, s % 2, h, off:QC], start=(kb == 0), stop=(kb >= KQ * qc),
                                         skip_group_check=True)
                    last.then_inc(used, 1)

                def iteration(b, p, q):
                    if b is not None:
                        score(b, 0)
                    for s in range(STEPS + 1):
                        if b is not None and s + 1 < STEPS:
                            score(b, s + 1)
                        if p is not None:
                            for kind, k in PREP.get(s, ()):
                                side_item(prep, bank_a, kind, k, p)
                        if q is not None:
                            for kind, k in POST.get(s, ()):
                                side_item(post, bank_b, kind, k, q)
                        if b is not None and s in DENOM_AT:
                            n = DENOM_AT[s]
                            fill(post, bank_b)
                            pe.wait_ge(copied, b * NSLOTS + n + 3)
                            pe.matmul(post.bank[:], spread[:, n // NQC % 2, :], sums[:, n % 2, :], start=True, stop=True)\
                              .then_inc(post.full, 1)
                        if b is not None and s < STEPS:
                            weigh_v(b, s)

                pe.wait_ge(weights, 16 * 11)
                pe.wait_ge(halved, 1)
                pe.wait_ge(tabled, 1)
                if shifted:
                    pe.wait_ge(ones_ready, 1)
                pe.sem_inc(used, 2)
                sequences(pe, iteration, bank_a, bank_b)
                if not shifted:
                    pe.wait_ge(seen_ready, 1)
                    for p in range(2):
                        pe.wait_ge(exped[p], NB * STEPS + 1)
                    for odd in range(2):
                        for c in range(2):
                            last = pe.matmul(s_tile[odd][:, c, :], spread[:, odd, :], seen[:, odd, c, :],
                                             start=True, stop=True)
                        last.then_inc(spread_seen, 1)
                    pe.wait_ge(in_range_ready, 1)
                    pe.matmul(prep.bank[:, 0:4], const["ones"][:], in_range[:], start=True, stop=True)\
                      .then_inc(range_summed, 1)

        @block.scalar
        def _(act):
            with only_if(act, flag):
                bank_a, bank_b = Uses(), Uses()

                def side_item(side, uses, kind, k, b):
                    n = uses.next() if kind in BANKED else None
                    if kind == "turn":
                        act.wait_ge(side.full, n)
                        g, c = (k // 2) % 2, k % 2
                        act.activation(side.xnT[:, c, g * QC:(g + 1) * QC], side.bank[:], ACT.Copy)\
                           .then_inc(side.free, 1)
                    if kind == "zturn":
                        act.wait_ge(side.full, n)
                        act.activation(side.zT[:, k * QC:(k + 1) * QC], side.bank[:], ACT.Copy)\
                           .then_inc(side.free, 1)
                    if kind == "gate_exp":
                        act.wait_ge(side.gap_ready, b + 1)
                        act.activation(side.gap[:], side.gap[:], ACT.Exp).then_inc(side.exp_ready, 1)
                    if kind == "high":
                        act.wait_ge(rotated, b * 4 + k + 1)
                        if not isinstance(b, int) or b * 4 + k > 0:
                            act.wait_ge(part_stored[0], (b * 4 + k) * 16)
                        act.activation(part[0][:], turned_qk[:], ACT.Copy).then_inc(part_ready[0], 1)
                    if kind == "mid":
                        act.wait_ge(rest_ready, b * 4 + k + 1)
                        if not isinstance(b, int) or b * 4 + k > 0:
                            act.wait_ge(part_stored[1], (b * 4 + k) * 16)
                        act.activation(part[1][:], rest[:], ACT.Copy).then_inc(part_ready[1], 1)

                def exps(b, s):
                    hg, qc, kb = SLOT_OF[s]
                    off = max(kb - KQ * qc, 0) * P
                    act.wait_ge(used, b * STEPS + s + 1)
                    for p in range(2):
                        act.wait_ge(scored[p], b * STEPS + s + 1)
                        act.activation(probs[:, s % 2, 2 * p:2 * p + 2, off:QC], s_tile[p][:, :, off:QC], ACT.Exp,
                                       scale=float(HD) ** -0.5).then_inc(exped[p], 1)

                def items(b, p, q, s):
                    if p is not None:
                        for kind, k in PREP.get(s, ()):
                            side_item(prep, bank_a, kind, k, p)
                    if q is not None:
                        for kind, k in POST.get(s, ()):
                            side_item(post, bank_b, kind, k, q)
                    if b is not None and s in DENOM_AT:
                        bank_b.next()

                def iteration(b, p, q):
                    for s in range(STEPS + 1):
                        if b is not None and s < STEPS:
                            exps(b, s)
                        if s > 0:
                            items(b, p, q, s - 1)
                    items(b, p, q, STEPS)

                for p in range(2):
                    act.sem_inc(exped[p], 1)
                sequences(act, iteration, bank_a, bank_b)

        @block.gpsimd
        def _(pool):
            with only_if(pool, flag):
                bank_a, bank_b = Uses(), Uses()

                def side_item(side, uses, kind, k, b):
                    if kind in BANKED:
                        uses.next()
                    if kind == "stats":
                        pool.wait_ge(side.moments_ready, b * side.norms + k + 1)
                        norm_rstd(pool, side.moments[k % 2], side.var_eps[:, k % 2], side.rstd[:, k % 2],
                                  const["eps"][:], const["minus_half"][:]).then_inc(side.rstd_ready, 1)
                    if kind == "bias":
                        pool.wait_ge(side.xn_ready, b * side.norms + 2)
                        pool.tensor_tensor(at(x, b % 3), at(x, b % 3), row_bcast(half_b[:], TS, [P, TS, D]),
                                           ALU.add).then_inc(side.biased, 1)
                    if kind == "high":
                        pool.wait_ge(side.free, uses.so_far() + 1)
                        if not isinstance(b, int) or b * 4 + k > 0:
                            pool.wait_ge(part_ready[0], b * 4 + k)
                        pool.tensor_tensor(turned_qk[:, 0, :], rope[:, 0, :], rope[:, 2, :], ALU.subtract)
                        pool.tensor_tensor(turned_qk[:, 1, :], rope[:, 1, :], rope[:, 3, :], ALU.add).then_inc(rotated, 1)
                    if kind == "mid":
                        pool.wait_ge(part_ready[0], b * 4 + k + 1)
                        if not isinstance(b, int) or b * 4 + k > 0:
                            pool.wait_ge(part_ready[1], b * 4 + k)
                        pool.tensor_tensor(rest[:], turned_qk[:], part[0][:], ALU.subtract).then_inc(rest_ready, 1)
                    if kind == "low":
                        pool.wait_ge(part_ready[1], b * 4 + k + 1)
                        if not isinstance(b, int) or b * 4 + k > 0:
                            pool.wait_ge(part_stored[2], (b * 4 + k) * 16)
                        pool.tensor_tensor(part[2][:], rest[:], part[1][:], ALU.subtract).then_inc(part_ready[2], 1)

                def iteration(b, p, q):
                    for s in range(STEPS + 1):
                        if p is not None:
                            for kind, k in PREP.get(s, ()):
                                side_item(prep, bank_a, kind, k, p)
                        if q is not None:
                            for kind, k in POST.get(s, ()):
                                side_item(post, bank_b, kind, k, q)
                        if b is not None and s in DENOM_AT:
                            n = DENOM_AT[s]
                            pool.wait_ge(post.free, bank_b.next() + 1)
                            of = seen[:, n // NQC % 2]
                            pool.tensor_tensor(of[:, 0, :], of[:, 0, :], sums[:, n % 2, :], ALU.add)
                            pool.tensor_tensor(of[:, 1, :], of[:, 1, :], recip[:], ALU.add).then_inc(checked, 1)

                pool.memset(identb[:], 0.0)
                pool.memset(mask[:], 0.0)
                pool.memset(spread[:], 0.0)
                pool.memset(seen[:], 0.0)
                pool.memset(v[:], 1.0)
                pool.iota(iota[:], pattern=[[1, NT]], base=0, channel_multiplier=0, allow_small_or_imprecise_dtypes=True)
                pool.drain()
                pool.affine_select(out=identb[:], in_=identb[:], compare_op=ALU.not_equal, fill=1.0,
                                   base=0, pattern=[[-1, P]], channel_multiplier=1)
                pool.affine_select(out=mask[:], in_=mask[:], compare_op=ALU.is_ge, fill=MASKED,
                                   base=0, pattern=[[-1, P]], channel_multiplier=1)
                for odd in range(2):
                    for j in range(HG):
                        part_of = spread[:, odd, 32 * j:32 * j + 32]
                        pool.affine_select(out=part_of, in_=part_of, compare_op=ALU.not_equal, fill=1.0,
                                           base=-(32 * j + HD - odd), pattern=[[0, 32]], channel_multiplier=1)
                pool.drain()
                pool.sem_inc(tabled, 1)
                sequences(pool, iteration, bank_a, bank_b)
                pool.drain()
                pool.sem_inc(seen_ready, 1)

        @block.vector
        def _(dve):
            with only_if(dve, flag):
                bank_a, bank_b = Uses(), Uses()

                def side_item(side, uses, kind, k, b):
                    n = uses.next() if kind in BANKED else None
                    xb = at(x, b % 3)
                    if kind == "stats":
                        dve.drain()
                        if side is prep and k == 0:
                            dve.wait_ge(x_loaded, b * 16 + 16)
                        g = k % 2
                        rows = lambda t: at(x, b % 3)[:, GT * g + t, :]
                        norm_stats(dve, rows, side.stats[g], side.moments[g]).then_inc(side.moments_ready, 1)
                    if kind == "norm":
                        g = k % 2
                        dve.wait_ge(side.rstd_ready, b * side.norms + k + 1)
                        before = uses.so_far()
                        if not isinstance(before, int) or before > 0:
                            dve.wait_ge(side.full, before)
                        rows = lambda t: at(x, b % 3)[:, GT * g + t, :]
                        norm_apply(dve, side.xn, rows, side.moments[g], side.rstd[:, g]).then_inc(side.xn_ready, 1)
                    if kind == "zg":
                        dve.wait_ge(side.full, n)
                        dve.tensor_copy(side.zg[:, 2 * k:2 * k + 2, :],
                                        side.bank[:, 0:2 * NZG].rearrange("p (t z) -> p t z", t=2)).then_inc(side.free, 1)
                    if kind == "route":
                        dve.drain()
                        for t in range(TS):
                            dve.max(side.best[:, t, :], side.zg[:, t, NZ:NZG])
                        dve.drain()
                        for t in range(TS):
                            dve.max_index(side.best_at[:, t, :], side.best[:, t, :], side.zg[:, t, NZ:NZG])
                        dve.tensor_tensor(side.gap[:], side.zg[:, :, NZ:NZ + NT],
                                          side.best[:, :, 0:1].to_broadcast([P, TS, NT]), ALU.subtract)\
                           .then_inc(side.gap_ready, 1)
                        dve.drain()
                        for j, chosen in ((0, side.c0), (1, side.c1)):
                            dve.tensor_tensor(chosen[:], row_bcast(iota[:], TS, [P, TS, NT]),
                                              side.best_at[:, :, j:j + 1].to_broadcast([P, TS, NT]), ALU.is_equal)
                        dve.drain()
                        dve.tensor_tensor(side.c0[:], side.c0[:], side.c1[:], ALU.add)
                    if kind == "weigh":
                        dve.drain()
                        dve.wait_ge(side.exp_ready, b + 1)
                        dve.tensor_tensor(side.c0[:], side.c0[:], side.gap[:], ALU.mult)
                        dve.drain()
                        dve.tensor_reduce(side.den[:, 0, :], side.c0[:], AX.X, ALU.add)
                        dve.drain()
                        dve.tensor_scalar(side.den[:, 1, :], side.den[:, 0, :], 0.0, None, ALU.is_equal)
                        dve.drain()
                        dve.tensor_tensor(side.den[:, 0, :], side.den[:, 0, :], side.den[:, 1, :], ALU.add)
                        dve.drain()
                        dve.reciprocal(side.den[:, 2, :], side.den[:, 0, :])
                        dve.drain()
                        dve.tensor_tensor(side.c0[:], side.c0[:], side.den[:, 2, :].unsqueeze(2)
                                          .to_broadcast([P, TS, NT]), ALU.mult)
                        dve.drain()
                        for t in range(TS):
                            z = side.zg[:, t, 0:NZ].rearrange("p (e r) -> p e r", r=RANK)
                            last = dve.tensor_tensor(z, z, side.c0[:, t, :].unsqueeze(2).to_broadcast([P, NT, RANK]),
                                                     ALU.mult)
                        last.then_inc(side.z_ready, 1)
                    if kind in ("y", "wo"):
                        if kind == "y":
                            dve.wait_ge(side.biased, b + 1)
                        dve.wait_ge(side.full, n)
                        tiles = xb[:, 2 * k:2 * k + 2, :]
                        dve.tensor_tensor(tiles, side.bank[:].rearrange("p (t d) -> p t d", t=2), tiles, ALU.add)\
                           .then_inc(side.free, 1)
                    if kind == "qk":
                        j, eo = k // 2, k % 2
                        g = j // 2
                        dve.wait_ge(side.full, n)
                        if not isinstance(b, int) or b * 4 + j > 0:
                            dve.wait_ge(rotated, b * 4 + j)
                        tok = slice(g * QC, (g + 1) * QC)
                        one, two = (cos, sin) if eo == 0 else (sin, cos)
                        dve.tensor_tensor(rope[:, 2 * eo, :], side.bank[:], one[:, tok], ALU.mult)
                        dve.tensor_tensor(rope[:, 2 * eo + 1, :], side.bank[:], two[:, tok], ALU.mult)\
                           .then_inc(side.free, 1)
                    if kind == "v":
                        dve.wait_ge(side.full, n)
                        if not isinstance(b, int) or b > 0:
                            dve.wait_ge(used, (b - 1) * STEPS + STEPS - TS + 2 * k + 4)
                        for t in range(2):
                            last = dve.tensor_copy(v_heads[:, 2 * k + t, :, 0:HD], side.bank[:, t * D:(t + 1) * D]
                                                   .rearrange("p (h w) -> p h w", w=HD))
                        last.then_inc(side.free, 1)

                def copy_sums(b, n):
                    dve.wait_ge(used, b * STEPS + SLOT_END[n] + 3)
                    if not isinstance(b, int) or b * NSLOTS + n >= 2:
                        dve.wait_ge(checked, b * NSLOTS + n - 1)
                    dve.tensor_copy(sums[:, n % 2, :], o_bank[n % 2][:]).then_inc(copied, 1)

                def divide(b, n):
                    k = bank_b.next()
                    dve.wait_ge(post.full, k)
                    if not isinstance(b, int) or b * NSLOTS + n > 0:
                        dve.wait_ge(checked, b * NSLOTS + n)
                    dve.reciprocal(recip[:], post.bank[:]).then_inc(post.free, 1)
                    dve.drain()
                    hg, qc = n // NQC, n % NQC
                    own = attn[:, hg // 2, qc * QC:(qc + 1) * QC]
                    if hg % 2 == 0:
                        dve.scalar_tensor_tensor(own, sums[:, n % 2, :], halves[:, 0:1], recip[:], ALU.mult, ALU.mult)\
                           .then_inc(attn_ready, 1)
                    else:
                        dve.scalar_tensor_tensor(attn_odd[:], sums[:, n % 2, :], halves[:, 1:2], recip[:],
                                                 ALU.mult, ALU.mult)
                        dve.drain()
                        dve.tensor_tensor(own, own, attn_odd[:], ALU.add).then_inc(attn_ready, 1)

                def iteration(b, p, q):
                    for s in range(STEPS + 1):
                        if b is not None and s in COPY_AT:
                            copy_sums(b, COPY_AT[s])
                        if p is not None:
                            for kind, k in PREP.get(s, ()):
                                side_item(prep, bank_a, kind, k, p)
                        if q is not None:
                            for kind, k in POST.get(s, ()):
                                side_item(post, bank_b, kind, k, q)
                        if b is not None and s in DENOM_AT:
                            divide(b, DENOM_AT[s])

                dve.wait_ge(weights, 16 * 11)
                dve.wait_ge(tabled, 1)
                for buf in (w_base, half_b):
                    dve.tensor_scalar(buf[:], buf[:], 0.5, None, ALU.mult)
                dve.drain()
                dve.sem_inc(halved, 1)
                dve.sem_inc(prep.free, 1)
                dve.sem_inc(post.free, 1)
                dve.sem_inc(copied, 2)
                if shifted:
                    dve.memset(k_rows[ROWS:n_rows], 1.0).then_inc(ones_ready, 1)
                sequences(dve, iteration, bank_a, bank_b)
                if not shifted:
                    for odd in range(2):
                        dve.wait_ge(spread_seen, odd + 1)
                        for c in range(2):
                            dve.tensor_scalar(sums[:, c, :], s_tile[odd][:, c, :], (D_LIMIT, INV_D_LIMIT)[c], None,
                                              ALU.is_le)
                        dve.drain()
                        last = dve.tensor_reduce(in_range[:, 2 * odd:2 * odd + 2], sums[:], AX.X, ALU.min)
                        if odd == 0:
                            dve.drain()
                    last.then_inc(in_range_ready, 1)
                    dve.wait_ge(range_summed, 1)
                    dve.tensor_scalar(out_of_range[:, 0:4], prep.bank[:, 0:4], float(P), None, ALU.is_lt)
                    dve.drain()
                    dve.tensor_reduce(out_of_range[:, 4:5], out_of_range[:, 0:4], AX.X, ALU.max)
                    dve.drain()
                    dve.tensor_copy(const["flag"][:, 2:3], out_of_range[:, 4:5])


def build(nc, io):
    with ExitStack() as nc_ctx:
        m = Pools(nc, nc_ctx, "c_")
        const = {
            "ident": m.sb("ident", [P, P]), "ones": m.sb("ones", [P, P]),
            "eps": m.sb("eps", [P, GT]), "minus_half": m.sb("minus_half", [P, GT]),
            "iota0": m.sb("iota0", [P, GT, E0]), "keep": m.sb("keep", [P, 2, E0]), "flag": m.sb("flag", [P, 3], I32),
        }
        built = m.sem("built")
        with nc.Block() as block:
            @block.gpsimd
            def _(pool):
                pool.memset(const["ident"][:], 0.0)
                pool.memset(const["ones"][:], 1.0)
                pool.memset(const["eps"][:], EPS)
                pool.memset(const["minus_half"][:], -0.5)
                pool.drain()
                pool.affine_select(out=const["ident"][:], in_=const["ident"][:], compare_op=ALU.not_equal, fill=1.0,
                                   base=0, pattern=[[-1, P]], channel_multiplier=1)
                pool.iota(const["iota0"][:], pattern=[[0, GT], [1, E0]], base=0, channel_multiplier=0,
                          allow_small_or_imprecise_dtypes=True).then_inc(built, 1)
                pool.wait_ge(built, 1)
        token_pass(nc, io, const, 0, False, io["x"], None, None)
        moe_pass(nc, io, const, 0, io["x"], io["x_moe"])
        token_pass(nc, io, const, 1, True, io["x"], io["x_moe"], io["x_mix"])
        moe_pass(nc, io, const, 1, io["x_mix"], io["x_mix"])
        sequence_pass(nc, io, const, False)
        row_max_pass(nc, io, const)
        sequence_pass(nc, io, const, True)


def _layouts(inp):
    import numpy as np

    c = np.ascontiguousarray

    def rows(a):
        return c(np.broadcast_to(a, (P, a.shape[-1])))

    def column(a):
        return c(a.reshape(-1, P).T)

    def pairs(w):
        return c(w.reshape(H, HD // 2, 2, D).transpose(2, 1, 0, 3).reshape(D, D).T)

    inv_freq = (10000.0 ** (-np.arange(0, HD, 2, dtype=np.float32) / HD)).astype(np.float32)
    angle = np.repeat(inv_freq, H)[:, None] * np.arange(S, dtype=np.float32)[None, :]
    return {
        "x": c(inp["L0_attn_x"].reshape(-1, D)),
        "gate0T": c(inp["L0_ffn_gate_w"].T),
        "w1T": c(inp["L0_ffn_w1"].transpose(0, 2, 1)), "w2T": c(inp["L0_ffn_w2"].transpose(0, 2, 1)),
        "b1": c(inp["L0_ffn_b1"].reshape(E0, DC, P).transpose(2, 0, 1)),
        "b2": c(np.broadcast_to(inp["L0_ffn_b2"], (P, E0, D))),
        "w_inT": c(inp["L0_attn_W_in"].T), "w_g": c(inp["L0_attn_W_g"]), "w_out": c(inp["L0_attn_W_out"]),
        "b_in": column(inp["L0_attn_b_in"]), "b_g": column(inp["L0_attn_b_g"]), "b_sp": column(inp["L0_attn_b_sp"]),
        "b_out": rows(inp["L0_attn_b_out"]), "norm_w": rows(inp["L0_attn_norm_w"]),
        "norm_b": rows(inp["L0_attn_norm_b"]),
        "w_agT": c(np.concatenate([inp["L1_ffn_lora_A"].reshape(NZ, D), inp["L1_ffn_gate_w"]]).T),
        "w_baseT": c(inp["L1_ffn_base_w"].T),
        "w_b": c(inp["L1_ffn_lora_B"].transpose(0, 2, 1).reshape(NZ, D)), "base_b": rows(inp["L1_ffn_base_b"]),
        "w_qT": pairs(inp["L1_attn_Wq"]), "w_kT": pairs(inp["L1_attn_Wk"]),
        "w_vT": c(inp["L1_attn_Wv"].T),
        "w_oT": c(inp["L1_attn_Wo"].T.reshape(NHG // 2, 2, HG, HD, D).transpose(0, 2, 1, 3, 4).reshape(D, D)),
        "halves": c(np.tile(np.repeat(np.eye(2, dtype=np.float32), HD, axis=0), (HG, 1))),
        "cos": np.cos(angle).astype(np.float32), "sin": np.sin(angle).astype(np.float32),
    }


def kernel(**inputs):
    import numpy as np
    import concourse.bacc as bacc
    from concourse.bass_utils import run_bass_kernel_spmd

    inputs = {name: np.asarray(a) for name, a in inputs.items()}
    shape = inputs["L0_attn_x"].shape
    tokens = shape[0] * shape[1]
    arrays = _layouts(inputs)
    nc = bacc.Bacc("TRN2", target_bir_lowering=False, num_devices=1)
    io = {name: nc.dram_tensor(name, a.shape, mybir.dt.from_np(a.dtype), kind="ExternalInput").ap()
          for name, a in arrays.items()}
    io["tokens"] = tokens
    io["cap"] = int(1.25 * tokens / E0)
    for name in ("x_moe", "x_mix"):
        io[name] = nc.dram_tensor(name, (tokens, D), F32).ap()
    io["parts"] = nc.dram_tensor("parts", (shape[0], 2, 3, 2, P, S), BF16).ap()
    io["shift"] = nc.dram_tensor("shift", (shape[0], 3, H, S), BF16).ap()
    io["out"] = nc.dram_tensor("out", (tokens, D), F32, kind="ExternalOutput").ap()
    build(nc, io)
    r = run_bass_kernel_spmd(nc, [arrays], core_ids=[0])
    return r.results[0]["out"].reshape(shape)
```
